# Optimizing a Trainium2 kernel written in Bass

```python
import numpy as np
import jax
import jax.numpy as jnp

def _softmax(x, axis=-1):
    return jax.nn.softmax(x, axis=axis)

def _gelu(x):
    return jax.nn.gelu(x, approximate=True)

def _silu(x):
    return jax.nn.silu(x)

def _sigmoid(x):
    return jax.nn.sigmoid(x)

def _layernorm(x, axis=-1, eps=1e-05):
    m = jnp.mean(x, axis=axis, keepdims=True)
    v = jnp.var(x, axis=axis, keepdims=True)
    return (x - m) / jnp.sqrt(v + eps)

def _scatter_add(tgt, idx, src, axis=0):
    return tgt.at[idx].add(src)

def _segment_sum(src, seg, n):
    return jax.ops.segment_sum(src, seg, n)
kernel_name = 'mk_gnn_resnorm_d1_gnn_r64_7aa8e9'

def setup_inputs(seed: int=0):
    np.random.seed(seed)
    _w = jnp.asarray

    def _rec_inputs():
        import jax
        import jax.numpy as jnp
        _gk = jax.random.key(seed)
        x = -0.000202 + 1 * jax.random.normal(jax.random.fold_in(_gk, 1), (50000, 128), jnp.float32)
        src = jax.random.randint(jax.random.fold_in(_gk, 2), (12500,), 0, 50000, jnp.int32)
        dst = jax.random.randint(jax.random.fold_in(_gk, 3), (12500,), 0, 50000, jnp.int32)
        _o = jnp.argsort(dst, stable=True)
        src = src[_o]
        dst = dst[_o]
        return (x, src, dst)
    x, src, dst = _rec_inputs()

    def _L0_gnn_setup():
        import jax, jax.numpy as jnp
        import numpy as np
        N_NODES = 50000
        N_EDGES = 12500
        NINP = 128
        D2 = 2 * NINP
        EPS = 1e-12

        def _l2norm(x):
            n = jnp.sqrt(jnp.sum(x * x, axis=-1, keepdims=True))
            return x / jnp.maximum(n, EPS)

        def _gcn_conv(x, W, b, src, dst, dinv):
            h = x @ W
            norm = dinv[src] * dinv[dst]
            agg = jax.ops.segment_sum(h[src] * norm[:, None], dst, num_segments=x.shape[0])
            agg = agg + (dinv * dinv)[:, None] * h
            return agg + b
        key = jax.random.key(seed)
        ks = jax.random.split(key, 11)
        s1 = 1.0 / np.sqrt(NINP)
        s2 = 1.0 / np.sqrt(D2)
        return {'node_embedding': jax.random.normal(ks[0], (N_NODES, NINP), jnp.float32), 'edge_index': jax.random.randint(ks[1], (2, N_EDGES), 0, N_NODES, dtype=jnp.int64), 'W1': jax.random.normal(ks[2], (NINP, D2), jnp.float32) * s1, 'b1': jnp.zeros((D2,), jnp.float32), 'Wf1': jax.random.normal(ks[3], (D2, D2), jnp.float32) * s2, 'bf1': jnp.zeros((D2,), jnp.float32), 'Wf2': jax.random.normal(ks[4], (D2, D2), jnp.float32) * s2, 'bf2': jnp.zeros((D2,), jnp.float32), 'W2': jax.random.normal(ks[5], (D2, NINP), jnp.float32) * s2, 'b2': jnp.zeros((NINP,), jnp.float32)}
    _L0_gnn_all = _L0_gnn_setup()
    _L0_gnn_in = {k: v for k, v in _L0_gnn_all.items() if k in ('W1', 'b1', 'Wf1', 'bf1', 'Wf2', 'bf2', 'W2', 'b2')}
    del _L0_gnn_all
    return {'x': x, 'src': src, 'dst': dst, 'L0_gnn_W1': _L0_gnn_in['W1'], 'L0_gnn_b1': _L0_gnn_in['b1'], 'L0_gnn_Wf1': _L0_gnn_in['Wf1'], 'L0_gnn_bf1': _L0_gnn_in['bf1'], 'L0_gnn_Wf2': _L0_gnn_in['Wf2'], 'L0_gnn_bf2': _L0_gnn_in['bf2'], 'L0_gnn_W2': _L0_gnn_in['W2'], 'L0_gnn_b2': _L0_gnn_in['b2']}

def reference(x, src, dst, L0_gnn_W1, L0_gnn_b1, L0_gnn_Wf1, L0_gnn_bf1, L0_gnn_Wf2, L0_gnn_bf2, L0_gnn_W2, L0_gnn_b2):
    import jax
    import jax.numpy as jnp

    def _L0_gnn_ref(node_embedding, edge_index, W1, b1, Wf1, bf1, Wf2, bf2, W2, b2):
        import jax, jax.numpy as jnp
        import numpy as np
        N_NODES = 50000
        N_EDGES = 12500
        NINP = 128
        D2 = 2 * NINP
        EPS = 1e-12

        def _l2norm(x):
            n = jnp.sqrt(jnp.sum(x * x, axis=-1, keepdims=True))
            return x / jnp.maximum(n, EPS)

        def _gcn_conv(x, W, b, src, dst, dinv):
            h = x @ W
            norm = dinv[src] * dinv[dst]
            agg = jax.ops.segment_sum(h[src] * norm[:, None], dst, num_segments=x.shape[0])
            agg = agg + (dinv * dinv)[:, None] * h
            return agg + b
        src, dst = (edge_index[0], edge_index[1])
        n = node_embedding.shape[0]
        deg = jax.ops.segment_sum(jnp.ones(src.shape[0], node_embedding.dtype), dst, num_segments=n) + 1.0
        dinv = jax.lax.rsqrt(deg)
        x = _gcn_conv(node_embedding, W1, b1, src, dst, dinv)
        x = _l2norm(x)

        def f(z):
            z1 = _gcn_conv(z, Wf1, bf1, src, dst, dinv)
            z1 = _l2norm(z1)
            return _gcn_conv(z1, Wf2, bf2, src, dst, dinv) + z
        k1 = f(x)
        k2 = f(x + 0.5 * k1)
        k3 = f(x + 0.5 * k2)
        k4 = f(x + k3)
        x = x + (k1 + 2.0 * k2 + 2.0 * k3 + k4) / 6.0
        return _gcn_conv(x, W2, b2, src, dst, dinv)
    edge_index = jnp.stack([src, dst])
    x = _layernorm(x + _L0_gnn_ref(x, edge_index, L0_gnn_W1, L0_gnn_b1, L0_gnn_Wf1, L0_gnn_bf1, L0_gnn_Wf2, L0_gnn_bf2, L0_gnn_W2, L0_gnn_b2), axis=-1)
    return x

_drawn_inputs = setup_inputs


def setup_inputs(seed=0):
    import zlib

    import numpy as np

    out = dict(_drawn_inputs(seed))
    spreads = {'L0_gnn_b1': (0.0, 0.389),
     'L0_gnn_bf1': (0.0, 0.1),
     'L0_gnn_bf2': (0.0, 0.1),
     'L0_gnn_b2': (0.0, 0.1)}
    factors = {}
    for name, (base, spread) in spreads.items():
        noise = np.random.default_rng([zlib.crc32(name.encode()), seed]).standard_normal(out[name].shape)
        drawn = base * np.exp(spread * noise) if base else spread * noise
        out[name] = jnp.asarray(drawn.astype(out[name].dtype))
    for name, factor in factors.items():
        out[name] = (out[name] * factor).astype(out[name].dtype)
    return out
```

```python
import concourse.bass as bass
from concourse import mybir
from contextlib import ExitStack


def bass_gnn_rk4_resnorm(
    nc: bass.Bass,
    x: bass.AP,
    src_pad: bass.AP,
    dst_pad: bass.AP,
    W1: bass.AP,
    b1: bass.AP,
    Wf1: bass.AP,
    bf1: bass.AP,
    Wf2: bass.AP,
    bf2: bass.AP,
    W2: bass.AP,
    b2: bass.AP,
    out: bass.AP,
):
    fp32 = mybir.dt.float32
    fp32r = mybir.dt.float32r
    bf16 = mybir.dt.bfloat16
    i32 = mybir.dt.int32
    ALU = mybir.AluOpType
    ACT = mybir.ActivationFunctionType
    AX = mybir.AxisListType

    P = 128
    N, D = x.shape
    H = W1.shape[1]
    KB = H // P
    G = 2
    LANES = 4
    ROWS = LANES * G * P
    ITERS = -(-N // ROWS)
    LAST_BASE = N - ROWS
    STEPS = 10
    SLOTS = STEPS * LANES
    LAG = 2
    EPS_NORM = 1e-12
    EPS_LN = 1e-5

    E_PAD = dst_pad.shape[0] - 2
    ET = E_PAD // P
    UNITS = ET // G
    SLOT_ROW0 = N
    N_PAD = -(-N // P) * P
    T_ROWS = SLOT_ROW0 + E_PAD
    SKIP = 1 << 20

    CONV1, F1, F2, OUT = "conv1", "f1", "f2", "out"

    def kind(s):
        return CONV1 if s == 0 else OUT if s == STEPS - 1 else F1 if s % 2 else F2

    COEF = {1: 0.5, 3: 0.5, 5: 1.0, 7: 1.0 / 3.0}
    NORM_STEPS = [0, 1, 3, 5, 7]
    Z_STEPS = [0, 2, 4, 6, 8]
    F1_STEPS = [1, 3, 5, 7]

    def nth(steps, s, l=0):
        return steps.index(s) * LANES + l

    NORMS = len(NORM_STEPS) * LANES + LANES

    def nth_root(s, l):
        return (len(NORM_STEPS) if s == STEPS - 1 else NORM_STEPS.index(s)) * LANES + l

    tables = [nc.dram_tensor(f"table{s}", (T_ROWS, D if s == 0 else H), fp32).ap() for s in range(STEPS)]
    node_row = nc.dram_tensor("node_row", (N_PAD, 1), i32).ap()
    seg_dram = nc.dram_tensor("seg_dram", (ET, P), bf16).ap()
    resid_dram = nc.dram_tensor("resid_dram", (E_PAD, D), fp32).ap()
    xb_dram = nc.dram_tensor("xb_dram", (E_PAD, H), fp32).ap()
    base_dram = [nc.dram_tensor(f"base_dram{n}", (E_PAD, H), fp32).ap() for n in range(2)]
    q_dram = nc.dram_tensor("q_dram", (E_PAD, H), fp32).ap()

    ctx = ExitStack()
    with ctx:
        def sb(name, shape, dt, c=ctx):
            return c.enter_context(nc.sbuf_tensor(name, shape, dt))

        def pb(name, shape, dt, c=ctx):
            return c.enter_context(nc.psum_tensor(name, shape, dt))

        def sem(name, c=ctx):
            return c.enter_context(nc.semaphore(name))

        w1 = [sb(f"w1_{p}", [P, 1, H], fp32r) for p in ("hi", "lo")]
        wf1 = [sb(f"wf1_{p}", [P, KB, H], fp32r) for p in ("hi", "lo")]
        wf2 = [sb(f"wf2_{p}", [P, KB, H], fp32r) for p in ("hi", "lo")]
        w2 = [sb(f"w2_{p}", [P, KB, D], fp32r) for p in ("hi", "lo")]
        ident = sb("ident", [P, P], fp32)
        bias_rows = sb("bias_rows", [64, 2, H], fp32r)
        ones_rows = sb("ones_rows", [64, P], fp32r)
        bf2_half = sb("bf2_half", [P, 1, H], fp32)
        b1_bc = sb("b1_bc", [P, H], fp32)
        bf1_bc = sb("bf1_bc", [P, H], fp32)
        b2_bc = sb("b2_bc", [P, 1, D], fp32)
        dinv = sb("dinv", [P, ET], fp32)
        dinv_half = sb("dinv_half", [P, ET], fp32)
        seg_col = sb("seg_col", [P, ET], fp32)
        src_row = sb("src_row", [P, ET], i32)
        self_idx = sb("self_idx", [P, ET], i32)
        out_idx = sb("out_idx", [P, ET], i32)

        weights = {0: w1, STEPS - 1: w2}
        for s in range(1, STEPS - 1):
            weights[s] = wf1 if s % 2 else wf2

        waited = sem("waited")

        with ExitStack() as c:
            w_raw = sb("w_raw", [P, 3 * KB * H], fp32, c)
            raw = {"w1": w_raw[:, 0:H].rearrange("p (b n) -> p b n", b=1)}
            at = H
            for name, n in (("wf1", H), ("wf2", H), ("w2", D)):
                raw[name] = w_raw[:, at:at + KB * n].rearrange("p (b n) -> p b n", b=KB)
                at += KB * n
            b_raw = sb("b_raw", [64, 2, H], fp32, c)
            bf2_bc = sb("bf2_bc", [P, H], fp32, c)
            dsti = sb("dsti", [ET, 3, P], i32, c)
            srci = sb("srci", [ET, P], i32, c)
            edge_no = sb("edge_no", [ET, P], fp32, c)
            slot_no = sb("slot_no", [ET, P], fp32, c)
            dstf = sb("dstf", [ET, 3, P], fp32, c)
            first = sb("first", [ET, P], fp32, c)
            last = sb("last", [ET, P], fp32, c)
            zeros = sb("zeros", [ET, P], fp32, c)
            seg = sb("seg", [ET, P], fp32, c)
            start = sb("start", [ET, P], fp32, c)
            tail = sb("tail", [ET, ET], fp32, c)
            ones_t = sb("ones_t", [ET, ET], fp32, c)
            before = sb("before", [ET, ET], fp32, c)
            carry = sb("carry", [ET, 1], fp32, c)
            deg = sb("deg", [ET, P], fp32, c)
            rt = sb("rt", [ET, P], fp32, c)
            di = sb("di", [ET, P], fp32, c)
            tmp = sb("tmp", [ET, P], fp32, c)
            rows = sb("rows", [ET, 6, P], fp32, c)
            seg_bf = sb("seg_bf", [ET, P], bf16, c)
            scat_val = sb("scat_val", [P, ET], i32, c)
            src_idx = sb("src_idx", [P, ET], i32, c)
            stage_i = sb("stage_i", [P, LANES], i32, c)
            stage_v = sb("stage_v", [P, LANES], i32, c)
            node_no = sb("node_no", [P, N_PAD // P], i32, c)
            ps_tail = pb("ps_tail", [ET, ET], fp32, c)
            ps_rows = pb("ps_rows", [P, 6, P], fp32, c)

            w_in = sem("w_in", c)
            e_in = sem("e_in", c)
            iotas = sem("iotas", c)
            b_zero = sem("b_zero", c)
            v = sem("v", c)
            tail_sum = sem("tail_sum", c)
            rooted = sem("rooted", c)
            rows_t = sem("rows_t", c)
            cols_done = sem("cols_done", c)
            map_init = sem("map_init", c)
            staged = sem("staged", c)
            scattered = sem("scattered", c)
            gathered = sem("gathered", c)
            taken = sem("taken", c)
            seg_out = sem("seg_out", c)

            block = c.enter_context(nc.Block())

            @block.sync
            def _(sp):
                sp.dma_start(dsti[:, 1, :], dst_pad[1:1 + E_PAD].rearrange("(t j) -> t j", j=P)).then_inc(e_in, 16)
                sp.dma_start(dsti[:, 0, :], dst_pad[0:E_PAD].rearrange("(t j) -> t j", j=P)).then_inc(e_in, 16)
                sp.dma_start(dsti[:, 2, :], dst_pad[2:2 + E_PAD].rearrange("(t j) -> t j", j=P)).then_inc(e_in, 16)
                sp.dma_start(srci[:, :], src_pad.rearrange("(t j) -> t j", j=P)).then_inc(e_in, 16)
                sp.dma_start(raw["w1"][:, 0, :], W1).then_inc(w_in, 16)
                sp.dma_start(raw["wf1"], Wf1.rearrange("(b p) n -> p b n", p=P)).then_inc(w_in, 16)
                sp.dma_start(raw["wf2"], Wf2.rearrange("(b p) n -> p b n", p=P)).then_inc(w_in, 16)
                sp.dma_start(raw["w2"], W2.rearrange("(b p) n -> p b n", p=P)).then_inc(w_in, 16)
                sp.wait_ge(b_zero, 1)
                for r in (0, 32):
                    sp.dma_start(b_raw[r:r + 1, 0, :], b1.rearrange("(a n) -> a n", a=1)).then_inc(w_in, 16)
                    sp.dma_start(b_raw[r:r + 1, 1, :], bf1.rearrange("(a n) -> a n", a=1)).then_inc(w_in, 16)
                for to, of in ((b1_bc[:, :], b1), (bf1_bc[:, :], bf1), (bf2_bc[:, :], bf2), (b2_bc[:, 0, :], b2)):
                    sp.dma_start(to, of.rearrange("(a n) -> a n", a=1).to_broadcast([P, of.shape[0]])).then_inc(w_in, 16)
                sp.wait_ge(map_init, 1)
                sp.dma_start(node_row.rearrange("(p c) a -> p (c a)", p=P), node_no[:, :]).then_inc(map_init, 16)
                sp.wait_ge(cols_done, 1)
                sp.dma_start(seg_dram, seg_bf[:, :]).then_inc(seg_out, 16)
                sp.wait_ge(seg_out, 16)

            @block.gpsimd
            def _(pool):
                pool.iota(edge_no[:, :], [[1, P]], base=0, channel_multiplier=P,
                          allow_small_or_imprecise_dtypes=True).then_inc(iotas, 1)
                pool.memset(zeros[:, :], 0.0).then_inc(iotas, 1)
                pool.memset(ones_t[:, :], 1.0).then_inc(iotas, 1)
                pool.memset(b_raw[:, :, :], 0.0).then_inc(b_zero, 1)
                pool.memset(ident[:, :], 0.0).then_inc(iotas, 1)
                pool.wait_ge(iotas, 4)
                pool.affine_select(out=ident[:, :], in_=ident[:, :], compare_op=ALU.not_equal, fill=1.0,
                                   base=0, pattern=[[-1, P]], channel_multiplier=1).then_inc(iotas, 1)
                pool.affine_select(out=before[:, :], in_=ones_t[:, :], compare_op=ALU.is_gt, fill=0.0,
                                   base=0, pattern=[[-1, ET]], channel_multiplier=1).then_inc(iotas, 1)
                pool.iota(slot_no[:, :], [[1, P]], base=SLOT_ROW0, channel_multiplier=P,
                          allow_small_or_imprecise_dtypes=True).then_inc(iotas, 1)
                pool.iota(node_no[:, :], [[1, N_PAD // P]], base=0,
                          channel_multiplier=N_PAD // P).then_inc(map_init, 1)
                pool.wait_ge(map_init, 17)
                pool.wait_ge(cols_done, 2)
                with pool.Fori(0, ET // LANES) as i:
                    pool.wait_ge(scattered, i * (16 * LANES))
                    pool.sem_inc(waited, 1)
                    nc.gpsimd.tensor_copy(stage_i[:, :], out_idx[:, bass.ds(i * LANES, LANES)]).then_inc(staged, 1)
                    nc.gpsimd.tensor_copy(stage_v[:, :], scat_val[:, bass.ds(i * LANES, LANES)]).then_inc(staged, 1)
                    pool.wait_ge(staged, i * 2 + 2)
                    pool.sem_inc(waited, 1)
                    for n in range(LANES):
                        pool.indirect_dma_start(
                            out=node_row, out_offset=bass.IndirectOffsetOnAxis(ap=stage_i[:, n:n + 1], axis=0),
                            in_=stage_v[:, n:n + 1], in_offset=None,
                            bounds_check=N_PAD - 1, oob_is_err=False).then_inc(scattered, 16)
                pool.wait_ge(scattered, 16 * ET)
                with pool.Fori(0, ET // LANES) as i:
                    nc.gpsimd.tensor_copy(stage_i[:, :], src_idx[:, bass.ds(i * LANES, LANES)]).then_inc(staged, 1)
                    pool.wait_ge(staged, i + (2 * (ET // LANES) + 1))
                    pool.sem_inc(waited, 1)
                    for n in range(LANES):
                        pool.indirect_dma_start(
                            out=stage_v[:, n:n + 1], out_offset=None,
                            in_=node_row, in_offset=bass.IndirectOffsetOnAxis(ap=stage_i[:, n:n + 1], axis=0),
                        ).then_inc(gathered, 16)
                    pool.wait_ge(gathered, i * (16 * LANES) + 16 * LANES)
                    pool.sem_inc(waited, 1)
                    nc.gpsimd.tensor_copy(src_row[:, bass.ds(i * LANES, LANES)], stage_v[:, :]).then_inc(taken, 1)
                    pool.wait_ge(taken, i + 1)
                    pool.sem_inc(waited, 1)

            @block.vector
            def _(dve):
                steps = [0]

                def step(ins):
                    steps[0] += 1
                    ins.then_inc(v, 1)
                    dve.wait_ge(v, steps[0])

                dve.wait_ge(e_in, 64)
                dve.wait_ge(iotas, 7)
                step(nc.vector.tensor_copy(dstf[:, :, :], dsti[:, :, :]))
                step(nc.vector.tensor_tensor(first[:, :], dstf[:, 1, :], dstf[:, 0, :], ALU.not_equal))
                step(nc.vector.tensor_tensor(last[:, :], dstf[:, 1, :], dstf[:, 2, :], ALU.not_equal))
                step(nc.vector.tensor_tensor_scan(seg[:, :], first[:, :], zeros[:, :], 0.0, ALU.add, ALU.add))
                step(nc.vector.tensor_tensor(tmp[:, :], first[:, :], edge_no[:, :], ALU.mult))
                step(nc.vector.tensor_tensor_scan(start[:, :], tmp[:, :], zeros[:, :], 0.0, ALU.max, ALU.max))
                nc.vector.tensor_scalar(tail[:, :], ident[0:ET, 0:ET], start[:, P - 1:P], None,
                                        ALU.mult).then_inc(v, 1)
                steps[0] += 1
                dve.wait_ge(tail_sum, 1)
                step(nc.vector.tensor_tensor(tail[:, :], ps_tail[:, :], before[:, :], ALU.mult))
                step(nc.vector.tensor_reduce(carry[:, :], tail[:, :], AX.X, ALU.max))
                step(nc.vector.tensor_scalar(start[:, :], start[:, :], carry[:, 0:1], None, ALU.max))
                step(nc.vector.tensor_tensor(deg[:, :], edge_no[:, :], start[:, :], ALU.subtract))
                nc.vector.tensor_scalar_add(deg[:, :], deg[:, :], 2.0).then_inc(v, 1)
                steps[0] += 1
                dve.wait_ge(rooted, 1)
                step(nc.vector.reciprocal(di[:, :], rt[:, :]))
                step(nc.vector.tensor_tensor(tmp[:, :], di[:, :], di[:, :], ALU.mult))
                step(nc.vector.tensor_tensor(tmp[:, :], tmp[:, :], deg[:, :], ALU.mult))
                step(nc.vector.tensor_scalar(tmp[:, :], tmp[:, :], -0.5, 1.5, ALU.mult, ALU.add))
                step(nc.vector.tensor_tensor(di[:, :], di[:, :], tmp[:, :], ALU.mult))
                step(nc.vector.tensor_scalar(tmp[:, :], dstf[:, 1, :], float(N), None, ALU.is_lt))
                step(nc.vector.tensor_tensor(last[:, :], last[:, :], tmp[:, :], ALU.mult))
                step(nc.vector.tensor_scalar_add(tmp[:, :], dstf[:, 1, :], -float(SKIP)))
                step(nc.vector.tensor_tensor(tmp[:, :], tmp[:, :], last[:, :], ALU.mult))
                step(nc.vector.tensor_scalar_add(tmp[:, :], tmp[:, :], float(SKIP)))
                step(nc.vector.tensor_copy(dstf[:, 2, :], srci[:, :]))
                step(nc.vector.tensor_scalar(dstf[:, 0, :], dstf[:, 1, :], float(N - 1), None, ALU.min))
                for n, row in enumerate((di[:, :], seg[:, :], dstf[:, 2, :], dstf[:, 0, :], tmp[:, :])):
                    nc.vector.tensor_copy(rows[:, n, 1:P - 1], row[:, 1:P - 1])
                    nc.vector.tensor_copy(rows[:, n, 0:1], row[:, P - 1:P])
                    step(nc.vector.tensor_copy(rows[:, n, P - 1:P], row[:, 0:1]))
                step(nc.vector.tensor_copy(rows[:, 5, :], slot_no[:, :]))
                nc.vector.tensor_copy(seg_bf[:, :], rows[:, 1, :]).then_inc(cols_done, 1)
                dve.wait_ge(rows_t, 1)
                nc.vector.tensor_copy(dinv[:, :], ps_rows[:, 0, 0:ET])
                nc.vector.tensor_scalar(dinv_half[:, :], ps_rows[:, 0, 0:ET], 0.5, None, ALU.mult)
                nc.vector.tensor_copy(seg_col[:, :], ps_rows[:, 1, 0:ET])
                nc.vector.tensor_copy(src_idx[:, :], ps_rows[:, 2, 0:ET])
                nc.vector.tensor_copy(self_idx[:, :], ps_rows[:, 3, 0:ET])
                nc.vector.tensor_copy(out_idx[:, :], ps_rows[:, 4, 0:ET])
                nc.vector.tensor_copy(scat_val[:, :], ps_rows[:, 5, 0:ET]).then_inc(cols_done, 1)
                dve.wait_ge(w_in, 12 * 16)
                for name, (hi, lo) in (("w1", w1), ("wf1", wf1), ("wf2", wf2), ("w2", w2)):
                    step(nc.vector.tensor_copy(hi[:, :, :], raw[name]))
                    step(nc.vector.tensor_tensor(lo[:, :, :], raw[name], hi[:, :, :].bitcast(fp32), ALU.subtract))
                step(nc.vector.tensor_copy(bias_rows[:, :, :], b_raw[:, :, :]))
                step(nc.vector.tensor_tensor(bias_rows[32:33, :, :], b_raw[32:33, :, :],
                                             bias_rows[32:33, :, :].bitcast(fp32), ALU.subtract))
                step(nc.vector.tensor_scalar(ones_rows[:, :], ident[0:64, :], 0.0, 1.0, ALU.mult, ALU.add))
                step(nc.vector.tensor_scalar(bf2_half[:, 0, :], bf2_bc[:, :], 0.5, None, ALU.mult))

            @block.scalar
            def _(act):
                act.wait_ge(v, 12)
                nc.scalar.activation(rt[:, :], deg[:, :], ACT.Sqrt).then_inc(rooted, 1)

            @block.tensor
            def _(pe):
                pe.wait_ge(v, 7)
                nc.tensor.matmul(ps_tail[:, :], ones_t[:, :], tail[:, :], start=True, stop=True).then_inc(tail_sum, 1)
                pe.wait_ge(cols_done, 1)
                for n in range(6):
                    mm = nc.tensor.transpose(ps_rows[:, n, 0:ET], rows[:, n, :], ident[0:ET, 0:ET])
                mm.then_inc(rows_t, 1)

        with ExitStack() as c:
            xt = sb("xt", [P, LANES, G, D], fp32, c)
            xres = sb("xres", [P, LANES, G, D], fp32, c)
            Z = [sb(f"Z{l}", [P, G, H], fp32, c) for l in range(LANES)]
            U = [sb(f"U{l}", [P, G, H], fp32, c) for l in range(LANES)]
            ZS = [sb(f"ZS{l}", [P, G, H], fp32, c) for l in range(LANES)]
            HI = [sb(f"HI{l}", [P, KB, G, P], fp32r, c) for l in range(LANES)]
            LO = [sb(f"LO{l}", [P, KB, G, P], fp32r, c) for l in range(LANES)]
            XB = [sb(f"XB{l}", [P, G, H], fp32, c) for l in range(LANES)]
            XQ = [sb(f"XQ{l}", [P, G, H], fp32, c) for l in range(LANES)]
            BA = [sb(f"BA{l}", [P, G, H], fp32, c) for l in range(LANES)]
            BB = [sb(f"BB{l}", [P, G, H], fp32, c) for l in range(LANES)]
            Y = [sb(f"Y{l}", [P, G, D], fp32, c) for l in range(LANES)]
            norm2 = [sb(f"norm2_{l}", [P, G], fp32, c) for l in range(LANES)]
            clamped = [sb(f"clamped{l}", [P, G], fp32, c) for l in range(LANES)]
            root = [sb(f"root{l}", [P, G], fp32, c) for l in range(LANES)]
            S = [sb(f"S{l}", [P, G], fp32, c) for l in range(LANES)]
            SL = [sb(f"SL{l}", [P, G], fp32, c) for l in range(LANES)]
            stats = [sb(f"stats{l}", [P, G, 6], fp32, c) for l in range(LANES)]
            mv = [sb(f"mv{l}", [P, G, 2], fp32, c) for l in range(LANES)]
            square = [sb(f"square{l}", [P, G, H], fp32, c) for l in range(LANES)]
            TB = [pb(f"TB{l}", [P, KB, G, P], fp32, c) for l in range(LANES)]
            MB = [pb(f"MB{l}", [P, G, H], fp32, c) for l in range(LANES)]

            x_in = sem("x_in", c)
            xres_in = sem("xres_in", c)
            t0_out = sem("t0_out", c)
            z_out = [sem(f"z_out{l}", c) for l in range(LANES)]
            zs_out = [sem(f"zs_out{l}", c) for l in range(LANES)]
            y_out = [sem(f"y_out{l}", c) for l in range(LANES)]
            transposed = sem("transposed", c)
            product = sem("product", c)
            high = sem("high", c)
            low = sem("low", c)
            u_done = sem("u_done", c)
            squared = sem("squared", c)
            clamp_done = sem("clamp_done", c)
            root_done = sem("root_done", c)
            s_done = sem("s_done", c)
            z_done = sem("z_done", c)
            zs_done = sem("zs_done", c)
            xb_done = sem("xb_done", c)
            xq_done = sem("xq_done", c)
            base_done = sem("base_done", c)
            q_done = sem("q_done", c)
            t_done = sem("t_done", c)
            resb_done = sem("resb_done", c)
            y_sum = sem("y_sum", c)
            stats_done = sem("stats_done", c)
            ln_root = sem("ln_root", c)
            y_done = sem("y_done", c)

            block = c.enter_context(nc.Block())

            def by_row(table, base):
                return table[bass.ds(base, ROWS), :].rearrange("(p l g) f -> p l g f", p=P, l=LANES)

            @block.sync
            def _(sp):
                def one_pass(i, base, next_base):
                    sp.wait_ge(x_in, (i + 1) * 16)
                    sp.dma_start(by_row(tables[0], base), xt[:, :, :, :]).then_inc(t0_out, 16)
                    sp.wait_ge(transposed, i * SLOTS + LANES)
                    sp.wait_ge(t0_out, (i + 1) * 16)
                    sp.dma_start(xt[:, :, :, :], by_row(x, next_base)).then_inc(x_in, 16)
                    sp.wait_ge(y_sum, i * LANES + LANES)
                    sp.dma_start(xres[:, :, :, :], by_row(x, base)).then_inc(xres_in, 16)
                    for s in range(STEPS):
                        for l in range(LANES):
                            if s in Z_STEPS:
                                sp.wait_ge(z_done, i * (len(Z_STEPS) * LANES) + nth(Z_STEPS, s, l) + 1)
                                sp.dma_start(by_row(tables[s + 1], base)[:, l], Z[l][:, :, :]).then_inc(z_out[l], 16)
                            elif s in F1_STEPS:
                                sp.wait_ge(zs_done, i * (len(F1_STEPS) * LANES) + nth(F1_STEPS, s, l) + LANES + 1)
                                sp.dma_start(by_row(tables[s + 1], base)[:, l], ZS[l][:, :, :]).then_inc(zs_out[l], 16)
                            else:
                                sp.wait_ge(y_done, i * LANES + l + 1)
                                sp.dma_start(by_row(out, base)[:, l], Y[l][:, :, :]).then_inc(y_out[l], 16)

                def stored(n):
                    for l in range(LANES):
                        sp.wait_ge(z_out[l], 16 * n * len(Z_STEPS))
                        sp.wait_ge(zs_out[l], 16 * n * len(F1_STEPS))
                        sp.wait_ge(y_out[l], 16 * n)

                sp.dma_start(xt[:, :, :, :], by_row(x, 0)).then_inc(x_in, 16)
                with sp.Fori(0, ITERS - 2) as i:
                    one_pass(i, i * ROWS, i * ROWS + ROWS)
                one_pass(ITERS - 2, (ITERS - 2) * ROWS, LAST_BASE)
                stored(ITERS - 1)
                one_pass(ITERS - 1, LAST_BASE, LAST_BASE)
                stored(ITERS)
                sp.wait_ge(x_in, (ITERS + 1) * 16)

            @block.tensor
            def _(pe):
                def transposes(i, k):
                    s, l = divmod(k, LANES)
                    if s == 0:
                        if l == 0:
                            pe.wait_ge(x_in, i * 16 + 16)
                    elif s - 1 in Z_STEPS:
                        pe.wait_ge(z_done, i * (len(Z_STEPS) * LANES) + nth(Z_STEPS, s - 1, l) + 1)
                    else:
                        pe.wait_ge(u_done, i * (len(F1_STEPS) * LANES) + nth(F1_STEPS, s - 1, l) + 1)
                    of = xt[:, l] if s == 0 else Z[l] if s - 1 in Z_STEPS else U[l]
                    for g in range(G):
                        for b in range(1 if s == 0 else KB):
                            mm = nc.tensor.transpose(TB[l][:, b, g, :], of[:, g, b * P:(b + 1) * P], ident[:, :])
                    mm.then_inc(transposed, 1)

                def products(i, k):
                    s, l = divmod(k, LANES)
                    if s == 0:
                        pe.wait_ge(y_sum, i * LANES + l + 1)
                    elif s - 1 in F1_STEPS:
                        pe.wait_ge(squared, i * (len(NORM_STEPS) * LANES) + nth(NORM_STEPS, s - 1, l) + 1)
                    pe.wait_ge(low, i * SLOTS + k + 1)
                    hi, lo = weights[s]
                    n = D if s == STEPS - 1 else H
                    for g in range(G):
                        if s == 0 or s in F1_STEPS:
                            nc.tensor.matmul(MB[l][:, g, 0:n], ones_rows[:, :], bias_rows[:, min(s, 1), :],
                                             start=True, stop=False)
                        terms = [(a, w, b) for b in range(1 if s == 0 else KB)
                                 for a, w in ((LO[l], hi), (HI[l], lo), (HI[l], hi))]
                        for m, (a, w, b) in enumerate(terms):
                            mm = nc.tensor.matmul(MB[l][:, g, 0:n], a[:, b, g, :], w[:, b, :],
                                                  start=(m == 0 and not (s == 0 or s in F1_STEPS)),
                                                  stop=(m == len(terms) - 1))
                    mm.then_inc(product, 1)

                for k in range(LAG):
                    transposes(0, k)
                with pe.Fori(0, ITERS) as i:
                    for k in range(SLOTS):
                        if k + LAG < SLOTS:
                            transposes(i, k + LAG)
                        else:
                            transposes(i + 1, k + LAG - SLOTS)
                        products(i, k)

            @block.scalar
            def _(act):
                def high_part(i, k):
                    s, l = divmod(k, LANES)
                    nb = 1 if s == 0 else KB
                    act.wait_ge(transposed, i * SLOTS + k + 1)
                    nc.scalar.copy(HI[l][:, 0:nb], TB[l][:, 0:nb]).then_inc(high, 1)

                def root_of(i, k):
                    s, l = divmod(k, LANES)
                    if s in NORM_STEPS or s == STEPS - 1:
                        act.wait_ge(clamp_done, i * NORMS + nth_root(s, l) + 1)
                        nc.scalar.activation(root[l][:, :], clamped[l][:, :], ACT.Sqrt).then_inc(root_done, 1)

                for k in range(LAG):
                    high_part(0, k)
                with act.Fori(0, ITERS) as i:
                    for k in range(SLOTS):
                        s, l = divmod(k, LANES)
                        if s in NORM_STEPS:
                            act.wait_ge(product, i * SLOTS + k + 1)
                            if s in F1_STEPS:
                                act.wait_ge(zs_done, i * (len(F1_STEPS) * LANES) + nth(F1_STEPS, s, l) + 1)
                                nc.scalar.copy(U[l][:, :, :], MB[l][:, :, :]).then_inc(u_done, 1)
                            for g in range(G):
                                sq = nc.scalar.activation(square[l][:, g, :], MB[l][:, g, :], ACT.Square,
                                                          accum_out=norm2[l][:, g:g + 1])
                            sq.then_inc(squared, 1)
                        if k + LAG < SLOTS:
                            high_part(i, k + LAG)
                        else:
                            high_part(i + 1, k + LAG - SLOTS)
                        if k >= 1:
                            root_of(i, k - 1)
                    root_of(i, SLOTS - 1)

            @block.vector
            def _(dve):
                NZ = len(Z_STEPS) * LANES
                NF = len(F1_STEPS) * LANES

                def low_part(i, k):
                    s, l = divmod(k, LANES)
                    nb = 1 if s == 0 else KB
                    dve.wait_ge(high, i * SLOTS + k + 1)
                    nc.vector.tensor_tensor(LO[l][:, 0:nb], TB[l][:, 0:nb], HI[l][:, 0:nb].bitcast(fp32),
                                            ALU.subtract).then_inc(low, 1)

                def early(i, k):
                    s, l = divmod(k, LANES)
                    if s in Z_STEPS and s > 0:
                        dve.wait_ge(product, i * SLOTS + k + 1)
                        dve.wait_ge(z_out[l], i * (16 * len(Z_STEPS)) + 16 * Z_STEPS.index(s))
                        dve.wait_ge(s_done, i * (len(NORM_STEPS) * LANES) + nth(NORM_STEPS, s - 1, l) + 1)
                        if s == 6:
                            dve.wait_ge(base_done, i * LANES + l + 1)
                        else:
                            dve.wait_ge(t_done, i * (4 * LANES) + {2: l, 4: LANES + l, 8: 2 * LANES + 2 * l + 1}[s] + 1)
                        base = {2: BA, 4: BB, 6: BA, 8: BB}[s][l]
                        for g in range(G):
                            ins = nc.vector.scalar_tensor_tensor(
                                out=Z[l][:, g, :], in0=MB[l][:, g, :], scalar=S[l][:, g:g + 1], in1=base[:, g, :],
                                op0=ALU.mult, op1=ALU.add)
                        ins.then_inc(z_done, 1)
                    elif s == 1:
                        dve.wait_ge(xb_done, i * LANES + l + 1)
                        nc.vector.scalar_tensor_tensor(out=BA[l][:, :, :], in0=Z[l][:, :, :], scalar=0.5,
                                                       in1=XB[l][:, :, :], op0=ALU.mult, op1=ALU.add).then_inc(t_done, 1)
                    elif s == 3:
                        dve.wait_ge(z_done, i * NZ + nth(Z_STEPS, 2, l) + 1)
                        nc.vector.scalar_tensor_tensor(out=BB[l][:, :, :], in0=Z[l][:, :, :], scalar=0.5,
                                                       in1=XB[l][:, :, :], op0=ALU.mult, op1=ALU.add).then_inc(t_done, 1)
                    elif s == 5:
                        dve.wait_ge(z_done, i * NZ + nth(Z_STEPS, 4, l) + 1)
                        dve.wait_ge(xq_done, i * LANES + l + 1)
                        nc.vector.tensor_tensor(BA[l][:, :, :], Z[l][:, :, :], XQ[l][:, :, :],
                                                ALU.add).then_inc(base_done, 1)
                    elif s == 7:
                        dve.wait_ge(z_done, i * NZ + nth(Z_STEPS, 6, l) + 1)
                        dve.wait_ge(q_done, i * LANES + l + 1)
                        nc.vector.scalar_tensor_tensor(out=BA[l][:, :, :], in0=XQ[l][:, :, :], scalar=4.0 / 3.0,
                                                       in1=Z[l][:, :, :], op0=ALU.mult, op1=ALU.add).then_inc(t_done, 1)
                    elif s == STEPS - 1:
                        dve.wait_ge(product, i * SLOTS + k + 1)
                        dve.wait_ge(resb_done, i + 1)
                        dve.wait_ge(y_out[l], i * 16)
                        nc.vector.scalar_tensor_tensor(out=Y[l][:, :, :], in0=MB[l][:, :, 0:D], scalar=0.5,
                                                       in1=xres[:, l], op0=ALU.mult, op1=ALU.add).then_inc(y_sum, 1)

                def middle(i, k):
                    s, l = divmod(k, LANES)
                    if s in NORM_STEPS:
                        dve.wait_ge(squared, i * (len(NORM_STEPS) * LANES) + nth(NORM_STEPS, s, l) + 1)
                        nc.vector.tensor_scalar(clamped[l][:, :], norm2[l][:, :], EPS_NORM ** 2,
                                                COEF.get(s, 1.0) ** -2, ALU.max, ALU.mult).then_inc(clamp_done, 1)
                    elif s == STEPS - 1:
                        dve.wait_ge(y_sum, i * LANES + LANES + l + 1)
                        for g in range(G):
                            ins = nc.vector.bn_stats(stats[l][:, g, :], Y[l][:, g, :])
                        ins.then_inc(stats_done, 1)
                        dve.wait_ge(stats_done, i * (2 * LANES) + 2 * l + 1)
                        dve.sem_inc(waited, 1)
                        for g in range(G):
                            ins = nc.vector.bn_aggr(mv[l][:, g, :], stats[l][:, g, :])
                        ins.then_inc(stats_done, 1)
                        dve.wait_ge(stats_done, i * (2 * LANES) + 2 * l + 2)
                        nc.vector.tensor_scalar_add(clamped[l][:, :], mv[l][:, :, 1], EPS_LN).then_inc(clamp_done, 1)
                    if s == 7:
                        dve.wait_ge(t_done, i * (4 * LANES) + 2 * LANES + 2 * l + 1)
                        nc.vector.scalar_tensor_tensor(out=BB[l][:, :, :], in0=XB[l][:, :, :], scalar=-10.0 / 3.0,
                                                       in1=BA[l][:, :, :], op0=ALU.mult, op1=ALU.add).then_inc(t_done, 1)

                def late(i, k):
                    s, l = divmod(k, LANES)
                    if s in NORM_STEPS:
                        n = i * (len(NORM_STEPS) * LANES) + nth(NORM_STEPS, s, l) + 1
                        dve.wait_ge(zs_done, i * NF + nth(F1_STEPS, max(s, 1), l) + 1)
                        dve.wait_ge(root_done, i * NORMS + nth_root(s, l) + 1)
                        nc.vector.reciprocal(S[l][:, :], root[l][:, :]).then_inc(s_done, 1)
                        if s == 0:
                            dve.wait_ge(s_done, n)
                            dve.wait_ge(z_out[l], i * (16 * len(Z_STEPS)))
                            for g in range(G):
                                ins = nc.vector.tensor_scalar(Z[l][:, g, :], MB[l][:, g, :], S[l][:, g:g + 1], None, ALU.mult)
                            ins.then_inc(z_done, 1)
                    elif s == STEPS - 1:
                        dve.wait_ge(root_done, i * NORMS + nth_root(s, l) + 1)
                        nc.vector.reciprocal(SL[l][:, :], root[l][:, :]).then_inc(ln_root, 1)
                        dve.wait_ge(ln_root, i * LANES + l + 1)
                        for g in range(G):
                            ins = nc.vector.tensor_scalar(Y[l][:, g, :], Y[l][:, g, :], mv[l][:, g, 0:1], SL[l][:, g:g + 1],
                                                          ALU.subtract, ALU.mult)
                        ins.then_inc(y_done, 1)

                nc.vector.memset(SL[0][:, :], 0.0).then_inc(y_sum, LANES)
                for k in range(LAG):
                    low_part(0, k)
                with dve.Fori(0, ITERS) as i:
                    for k in range(SLOTS):
                        if k + LAG < SLOTS:
                            early(i, k)
                            low_part(i, k + LAG)
                        else:
                            early(i, k)
                            low_part(i + 1, k + LAG - SLOTS)
                        middle(i, k)
                        if k >= 1:
                            late(i, k - 1)
                    late(i, SLOTS - 1)

            @block.gpsimd
            def _(pool):
                pool.memset(stats[0][:, :, :], 0.0).then_inc(zs_done, LANES)
                with pool.Fori(0, ITERS) as i:
                    for k in range(SLOTS):
                        s, l = divmod(k, LANES)
                        if s == 0:
                            pool.wait_ge(z_done, i * (len(Z_STEPS) * LANES) + l + 1)
                            nc.gpsimd.tensor_tensor(XB[l][:, :, :], Z[l][:, :, :],
                                                    bf2_half[:, :, :].to_broadcast([P, G, H]), ALU.add).then_inc(xb_done, 1)
                            pool.wait_ge(xb_done, i * LANES + l + 1)
                            nc.gpsimd.tensor_tensor(XQ[l][:, :, :], XB[l][:, :, :],
                                                    bf2_half[:, :, :].to_broadcast([P, G, H]), ALU.add).then_inc(xq_done, 1)
                        elif s in F1_STEPS:
                            n = nth(F1_STEPS, s, l)
                            pool.wait_ge(u_done, i * (len(F1_STEPS) * LANES) + n + 1)
                            pool.wait_ge(s_done, i * (len(NORM_STEPS) * LANES) + nth(NORM_STEPS, s, l) + 1)
                            pool.wait_ge(zs_out[l], i * (16 * len(F1_STEPS)) + 16 * F1_STEPS.index(s))
                            nc.gpsimd.tensor_tensor(ZS[l][:, :, :], U[l][:, :, :],
                                                    S[l][:, :].unsqueeze(2).to_broadcast([P, G, H]),
                                                    ALU.mult).then_inc(zs_done, 1)
                            if s == 5:
                                pool.wait_ge(base_done, i * LANES + l + 1)
                                nc.gpsimd.tensor_tensor(XQ[l][:, :, :], BA[l][:, :, :], BB[l][:, :, :],
                                                        ALU.add).then_inc(q_done, 1)
                        elif s == 6 and l == 0:
                            pool.wait_ge(xres_in, i * 16 + 16)
                            nc.gpsimd.tensor_tensor(xres[:, :, :, :].rearrange("p l g f -> p (l g) f"),
                                                    xres[:, :, :, :].rearrange("p l g f -> p (l g) f"),
                                                    b2_bc[:, :, :].to_broadcast([P, LANES * G, D]), ALU.add).then_inc(resb_done, 1)

        with ExitStack() as c:
            ZT = sb("ZT", [P, ET, H], fp32, c)
            seg_bc = sb("seg_bc", [P, ET * P], bf16, c)
            CR = [sb(f"CR{g}", [1, H], fp32, c) for g in range(G)]
            idx = [sb(f"idx{p}", [P, G], i32, c) for p in range(2)]
            oidx = [sb(f"oidx{p}", [P, G], i32, c) for p in range(2)]
            GA = [sb(f"GA{p}", [P, G, H], fp32, c) for p in range(2)]
            GA0 = [GA[p][:, :, 0:D] for p in range(2)]
            GH = [sb(f"GH{p}", [P, G, H], fp32r, c) for p in range(2)]
            GL = [sb(f"GL{p}", [P, G, H], fp32r, c) for p in range(2)]
            SM = [sb(f"SM{p}", [P, G, P], fp32r, c) for p in range(2)]
            M0 = [sb(f"M0_{p}", [1, G, P], fp32, c) for p in range(2)]
            WB = [sb(f"WB{p}", [P, G, H], fp32, c) for p in range(2)]
            EH = [sb(f"EH{p}", [P, KB, G, P], fp32r, c) for p in range(2)]
            EL = [sb(f"EL{p}", [P, KB, G, P], fp32r, c) for p in range(2)]
            UB = [sb(f"UB{p}", [P, G, H], fp32, c) for p in range(2)]
            ZN = [sb(f"ZN{p}", [P, G, H], fp32, c) for p in range(2)]
            SQ = [sb(f"SQ{p}", [P, G, H], fp32, c) for p in range(2)]
            BI = [sb(f"BI{p}", [P, G, H], fp32, c) for p in range(2)]
            AX_ = [sb(f"AX{p}", [P, G, H], fp32, c) for p in range(2)]
            BO = [sb(f"BO{p}", [P, G, H], fp32, c) for p in range(2)]
            XO = [sb(f"XO{p}", [P, G, H], fp32, c) for p in range(2)]
            RI = [AX_[p][:, :, 0:D] for p in range(2)]
            Y2 = [sb(f"Y2_{p}", [P, G, D], fp32, c) for p in range(2)]
            en2 = [sb(f"en2_{p}", [P, G], fp32, c) for p in range(2)]
            ecl = [sb(f"ecl{p}", [P, G], fp32, c) for p in range(2)]
            ert = [sb(f"ert{p}", [P, G], fp32, c) for p in range(2)]
            eS = [sb(f"eS{p}", [P, G], fp32, c) for p in range(2)]
            eSD = [sb(f"eSD{p}", [P, G], fp32, c) for p in range(2)]
            est = [sb(f"est{p}", [P, G, 6], fp32, c) for p in range(2)]
            emv = [sb(f"emv{p}", [P, G, 2], fp32, c) for p in range(2)]
            AB = [pb(f"AB{p}", [P, G, 512], fp32, c) for p in range(2)]
            TB2 = [pb(f"TB2_{p}", [P, KB, G, P], fp32, c) for p in range(2)]
            MB2 = [pb(f"MB2_{p}", [P, G, H], fp32, c) for p in range(2)]

            seg_in = sem("seg_in", c)
            start_idx = sem("start_idx", c)
            start_x = [sem(f"start_x{p}", c) for p in range(2)]
            start_res = sem("start_res", c)
            res_out = [sem(f"res_out{p}", c) for p in range(2)]
            idx_staged = sem("idx_staged", c)
            src_in = [sem(f"src_in{p}", c) for p in range(2)]
            g_high = sem("g_high", c)
            g_low = sem("g_low", c)
            same = sem("same", c)
            goes_on = sem("goes_on", c)
            summed = sem("summed", c)
            carried = sem("carried", c)
            own_added = sem("own_added", c)
            e_transposed = sem("e_transposed", c)
            e_high = sem("e_high", c)
            e_low = sem("e_low", c)
            e_product = sem("e_product", c)
            e_early = sem("e_early", c)
            e_squared = sem("e_squared", c)
            e_clamped = sem("e_clamped", c)
            e_root = sem("e_root", c)
            e_recip = sem("e_recip", c)
            e_scale = sem("e_scale", c)
            e_own = sem("e_own", c)
            ztil = sem("ztil", c)
            rk_step = sem("rk_step", c)
            rk_done = sem("rk_done", c)
            y2_done = sem("y2_done", c)
            zt_out = [sem(f"zt_out{p}", c) for p in range(2)]
            bo_out = [sem(f"bo_out{p}", c) for p in range(2)]
            xo_out = [sem(f"xo_out{p}", c) for p in range(2)]
            bi_in = [sem(f"bi_in{p}", c) for p in range(2)]
            ax_in = [sem(f"ax_in{p}", c) for p in range(2)]
            scat_idx = sem("scat_idx", c)
            scat = [sem(f"scat{p}", c) for p in range(2)]
            x1_done = sem("x1_done", c)

            block = c.enter_context(nc.Block())

            LEAD, FIRST, BODY = 4, 1, (UNITS - 6) // 2 * 2

            def positions(eng, at):
                for u in range(-LEAD, FIRST):
                    at(u, u % 2, lambda off, u=u: 0 <= u + off < UNITS)
                with eng.Fori(0, BODY // 2) as i:
                    for n in range(2):
                        at(i * 2 + (FIRST + n), (FIRST + n) % 2, lambda off: True)
                for u in range(FIRST + BODY, UNITS + 1):
                    at(u, u % 2, lambda off, u=u: 0 <= u + off < UNITS)

            def wait(eng, s_, value):
                if not isinstance(value, int) or value > 0:
                    eng.wait_ge(s_, value)

            def wait_apart(eng, s_, value):
                if not isinstance(value, int) or value > 0:
                    eng.wait_ge(s_, value)
                    eng.sem_inc(waited, 1)

            def slot_rows(t, u, first=SLOT_ROW0):
                return t[bass.ds(u * (G * P) + first, G * P), :].rearrange("(g p) f -> p g f", p=P)

            HALF = UNITS // 2
            NORM_L = [0] + F1_STEPS
            RK_L = [0, 2, 4, 6]
            BASE_IO = {0: (None, 0), 2: (0, 1), 4: (1, 0), 6: (0, 1), 8: (1, None)}

            def done_before(layers, s):
                return sum(1 for x_ in layers if x_ < s) * HALF

            BI_L, AX_L, BO_L, XO_L = [2, 4, 6, 8], [2, 4, 6, 9], [0, 2, 4, 6], [0, 4]

            @block.sync
            def _(sp):
                sp.dma_start(seg_bc[:, :], seg_dram.rearrange("(a t) p -> a (t p)", a=1).to_broadcast([P, ET * P])).then_inc(seg_in, 16)

                def start(i, p):
                    u = i * 2 + p
                    sp.wait_ge(ztil, i * 2 + (p + 1))
                    sp.dma_start(slot_rows(tables[0], u), ZT[:, bass.ds(u * G, G), 0:D]).then_inc(zt_out[p], 16)
                    sp.wait_ge(start_res, i * 2 + (p + 1))
                    sp.dma_start(slot_rows(resid_dram, u, 0), Y2[p][:, :, :]).then_inc(res_out[p], 16)

                with sp.Fori(0, HALF) as i:
                    for p in range(2):
                        start(i, p)
                for p in range(2):
                    sp.wait_ge(res_out[p], 16 * HALF)
                for s in range(STEPS):
                    for p in range(2):
                        wait(sp, bo_out[p], 16 * done_before(BO_L, s))
                        wait(sp, xo_out[p], 16 * done_before(XO_L, s))

                    def loads(u, p):
                        if s in BI_L:
                            sp.dma_start(BI[p][:, :, :], slot_rows(base_dram[BASE_IO[s][0]], u, 0)).then_inc(bi_in[p], 16)
                        if s in (2, 4, 6):
                            sp.dma_start(AX_[p][:, :, :], slot_rows(q_dram if s == 6 else xb_dram, u, 0)).then_inc(ax_in[p], 16)
                        if s == STEPS - 1:
                            sp.dma_start(RI[p], slot_rows(resid_dram, u, 0)).then_inc(ax_in[p], 16)

                    def stores(u, p):
                        q = u + s * UNITS
                        if s < STEPS - 1:
                            sp.wait_ge(ztil, q + (UNITS + 1))
                            sp.dma_start(slot_rows(tables[s + 1], u), ZT[:, bass.ds(u * G, G), :]).then_inc(zt_out[p], 16)
                        if s in RK_L:
                            sp.wait_ge(rk_done, u + (RK_L.index(s) * UNITS + 1))
                            sp.dma_start(slot_rows(base_dram[BASE_IO[s][1]], u, 0), BO[p][:, :, :]).then_inc(bo_out[p], 16)
                            if s in XO_L:
                                sp.dma_start(slot_rows(q_dram if s else xb_dram, u, 0), XO[p][:, :, :]).then_inc(xo_out[p], 16)
                        if s == STEPS - 1:
                            sp.wait_ge(e_early, q + 1)

                    loads(0, 0)
                    loads(1, 1)
                    with sp.Fori(0, HALF - 1) as i:
                        for p in range(2):
                            stores(i * 2 + p, p)
                            if s == 8:
                                sp.wait_ge(e_early, i * 2 + (p + s * UNITS + 1))
                            loads(i * 2 + (p + 2), p)
                    for p in range(2):
                        stores(UNITS - 2 + p, p)
                for p in range(2):
                    sp.wait_ge(zt_out[p], 16 * HALF * STEPS)

            @block.gpsimd
            def _(pool):
                pool.memset(CR[0][:, :], 0.0).then_inc(start_idx, 1)
                pool.memset(CR[1][:, :], 0.0).then_inc(carried, 1)

                def start_gather(i, p):
                    u = i * 2 + p
                    wait_apart(pool, ztil, i * 2 + p - 1 if isinstance(i, int) else i * 2 + (p - 1))
                    wait_apart(pool, start_res, i * 2 + p - 1 if isinstance(i, int) else i * 2 + (p - 1))
                    nc.gpsimd.tensor_copy(idx[p][:, :], self_idx[:, bass.ds(u * G, G)]).then_inc(start_idx, 1)
                    wait_apart(pool, start_idx, i * 2 + (p + 2))
                    for g in range(G):
                        pool.indirect_dma_start(out=GA0[p][:, g, :], out_offset=None, in_=x,
                                                in_offset=bass.IndirectOffsetOnAxis(ap=idx[p][:, g:g + 1], axis=0)
                                                ).then_inc(start_x[p], 16)

                def start_residual(i, p):
                    pool.wait_ge(start_x[p], i * 32 + 32)
                    wait(pool, res_out[p], i * 16)
                    nc.gpsimd.tensor_tensor(Y2[p][:, :, :], GA0[p][:, :, :], b2_bc[:, :, :].to_broadcast([P, G, D]),
                                            ALU.add).then_inc(start_res, 1)

                start_gather(0, 0)
                start_gather(0, 1)
                with pool.Fori(1, HALF) as i:
                    for p in range(2):
                        start_residual(i - 1, p)
                        start_gather(i, p)
                for p in range(2):
                    start_residual(HALF - 1, p)

                for s in range(STEPS):
                    w = D if s == 0 else H
                    for p in range(2):
                        pool.wait_ge(zt_out[p], 16 * HALF * (s + 1))

                    def gather(u, p):
                        q = u + s * UNITS
                        wait_apart(pool, g_low, q - 1)
                        nc.gpsimd.tensor_copy(idx[p][:, :], src_row[:, bass.ds(u * G, G)]).then_inc(idx_staged, 1)
                        wait_apart(pool, idx_staged, q + 1)
                        for g in range(G):
                            pool.indirect_dma_start(out=GA[p][:, g, 0:w], out_offset=None, in_=tables[s],
                                                    in_offset=bass.IndirectOffsetOnAxis(ap=idx[p][:, g:g + 1], axis=0)
                                                    ).then_inc(src_in[p], 16)

                    def scatter(u, p):
                        wait_apart(pool, scat[p], (u - p) * 16)
                        nc.gpsimd.tensor_copy(oidx[p][:, :], out_idx[:, bass.ds(u * G, G)]).then_inc(scat_idx, 1)
                        wait_apart(pool, scat_idx, u + 1)
                        wait_apart(pool, y2_done, u + 1)
                        for g in range(G):
                            pool.indirect_dma_start(out=out, out_offset=bass.IndirectOffsetOnAxis(ap=oidx[p][:, g:g + 1], axis=0),
                                                    in_=Y2[p][:, g, :], in_offset=None,
                                                    bounds_check=N - 1, oob_is_err=False).then_inc(scat[p], 16)

                    def at(u, p, there):
                        if s == STEPS - 1 and there(-1):
                            scatter(u - 1, 1 - p)
                        if there(4):
                            gather(u + 4, p)

                    positions(pool, at)
                for p in range(2):
                    pool.wait_ge(scat[p], 32 * HALF)

            @block.tensor
            def _(pe):
                for s in range(STEPS):
                    w = D if s == 0 else H
                    n = D if s == STEPS - 1 else H
                    hi, lo = weights[s]
                    nb = 1 if s == 0 else KB

                    def sums(u, p, g):
                        nc.tensor.matmul(AB[p][:, g, 0:w], SM[p][:, g, :], GH[p][:, g, 0:w], start=True, stop=False)
                        nc.tensor.matmul(AB[p][:, g, 0:w], SM[p][:, g, :], GL[p][:, g, 0:w], start=False, stop=False)

                    def carried_in(u, p, g):
                        pe.wait_ge(carried, (u + s * UNITS) * 2 + (g + 1))
                        nc.tensor.matmul(AB[p][:, g, 0:w], M0[p][0:1, g, :], CR[1 - g][0:1, 0:w],
                                         start=False, stop=True).then_inc(summed, 1)

                    def transposes(u, p):
                        pe.wait_ge(own_added, u + (s * UNITS + 1))
                        for g in range(G):
                            for b in range(nb):
                                mm = nc.tensor.transpose(TB2[p][:, b, g, :], WB[p][:, g, b * P:(b + 1) * P], ident[:, :])
                        mm.then_inc(e_transposed, 1)

                    def products(u, p, g):
                        q = u + s * UNITS
                        if g == 0:
                            pe.wait_ge(e_low, q + 1)
                            wait(pe, e_early, q - 1)
                        terms = [(a, w_, b) for b in range(nb)
                                 for a, w_ in ((EL[p], hi), (EH[p], lo), (EH[p], hi))]
                        for m, (a, w_, b) in enumerate(terms):
                            mm = nc.tensor.matmul(MB2[p][:, g, 0:n], a[:, b, g, :], w_[:, b, :],
                                                  start=m == 0, stop=m == len(terms) - 1)
                        if g == G - 1:
                            mm.then_inc(e_product, 1)

                    def at(u, p, there):
                        if there(0):
                            products(u, p, 0)
                        if there(1):
                            transposes(u + 1, 1 - p)
                        if there(2):
                            q = u + (s * UNITS + 2)
                            pe.wait_ge(g_low, q + 1)
                            pe.wait_ge(same, q + 1)
                            pe.wait_ge(goes_on, q + 1)
                            wait(pe, own_added, q - 1)
                            wait(pe, carried, q * 2 - 1)
                            sums(u + 2, p, 0)
                            carried_in(u + 2, p, 0)
                            sums(u + 2, p, 1)
                        if there(0):
                            products(u, p, 1)
                        if there(2):
                            carried_in(u + 2, p, 1)

                    positions(pe, at)

            @block.scalar
            def _(act):
                act.wait_ge(seg_in, 16)
                with act.Fori(0, HALF) as i:
                    for p in range(2):
                        wait_apart(act, start_x[p], i * 32 + 32)
                        for g in range(G):
                            ins = nc.scalar.activation(ZT[:, bass.ds((i * 2 + p) * G + g, 1), 0:D].rearrange("p a f -> p (a f)"),
                                                       GA0[p][:, g, :], ACT.Copy,
                                                       scale=dinv[:, bass.ds((i * 2 + p) * G + g, 1)])
                        ins.then_inc(ztil, 1)
                for s in range(STEPS):
                    w = D if s == 0 else H
                    nb = 1 if s == 0 else KB

                    def source_high(u, p):
                        act.wait_ge(src_in[p], (u - p) * 16 + (s * HALF + 1) * 32)
                        nc.scalar.copy(GH[p][:, :, 0:w], GA[p][:, :, 0:w]).then_inc(g_high, 1)

                    def continued(u, p):
                        wait_apart(act, summed, (u + s * UNITS) * 2 - 2)
                        nc.scalar.activation(M0[p][:, :, :].rearrange("a g p -> a (g p)"),
                                             seg_bc[0:1, bass.ds(u * (G * P), G * P)],
                                             ACT.Relu, scale=-1.0, bias=1.0).then_inc(goes_on, 1)

                    def keep(u, p, g):
                        act.wait_ge(summed, (u + s * UNITS) * 2 + (g + 1))
                        nc.scalar.copy(CR[g][0:1, 0:w], AB[p][0:1, g, 0:w]).then_inc(carried, 1)

                    def scaled(u, p):
                        q = u + s * UNITS
                        if s in NORM_L:
                            wait_apart(act, e_scale, u + (NORM_L.index(s) * UNITS + 1))
                        else:
                            wait_apart(act, e_early, q + 1)
                        for g in range(G):
                            if s in F1_STEPS:
                                of, by = UB[p][:, g, :], eSD[p][:, g:g + 1]
                            else:
                                of, by = ZN[p][:, g, :], dinv[:, bass.ds(u * G + g, 1)]
                            ins = nc.scalar.activation(ZT[:, bass.ds(u * G + g, 1), :].rearrange("p a f -> p (a f)"),
                                                       of, ACT.Copy, scale=by)
                        ins.then_inc(ztil, 1)

                    def at(u, p, there):
                        o = 1 - p
                        if there(1):
                            act.wait_ge(e_transposed, u + (s * UNITS + 2))
                            nc.scalar.copy(EH[o][:, 0:nb], TB2[o][:, 0:nb]).then_inc(e_high, 1)
                        if there(-1) and (s in NORM_L or s == STEPS - 1):
                            act.wait_ge(e_clamped, u + (NORM_L + [STEPS - 1]).index(s) * UNITS)
                            nc.scalar.activation(ert[o][:, :], ecl[o][:, :], ACT.Sqrt).then_inc(e_root, 1)
                        if there(2):
                            keep(u + 2, p, 0)
                        if there(3):
                            source_high(u + 3, o)
                            continued(u + 3, o)
                        if there(2):
                            keep(u + 2, p, 1)
                        if there(-1) and s < STEPS - 1:
                            scaled(u - 1, o)
                        if there(0) and s in NORM_L:
                            act.wait_ge(e_early, u + (s * UNITS + 1))
                            for g in range(G):
                                ins = nc.scalar.activation(SQ[p][:, g, :], UB[p][:, g, :], ACT.Square,
                                                           accum_out=en2[p][:, g:g + 1])
                            ins.then_inc(e_squared, 1)

                    positions(act, at)

            @block.vector
            def _(dve):
                dve.wait_ge(seg_in, 16)
                for s in range(STEPS):
                    w = D if s == 0 else H
                    nb = 1 if s == 0 else KB

                    def source_low(u, p):
                        dve.wait_ge(g_high, u + (s * UNITS + 1))
                        nc.vector.tensor_tensor(GL[p][:, :, 0:w], GA[p][:, :, 0:w], GH[p][:, :, 0:w].bitcast(fp32),
                                                ALU.subtract).then_inc(g_low, 1)

                    def matrices(u, p):
                        wait_apart(dve, summed, (u + s * UNITS) * 2 - 2)
                        for g in range(G):
                            ins = nc.vector.tensor_scalar(SM[p][:, g, :], seg_bc[:, bass.ds(u * (G * P) + g * P, P)],
                                                          seg_col[:, bass.ds(u * G + g, 1)], None, ALU.is_equal)
                        ins.then_inc(same, 1)

                    def add_own(u, p):
                        q = u + s * UNITS
                        dve.wait_ge(carried, q * 2 + 3)
                        wait(dve, e_transposed, q - 1)
                        dve.wait_ge(ztil, q + 1)
                        nc.vector.tensor_tensor(WB[p][:, :, 0:w], AB[p][:, :, 0:w], ZT[:, bass.ds(u * G, G), 0:w],
                                                ALU.add).then_inc(own_added, 1)

                    def early(u, p):
                        q = u + s * UNITS
                        dve.wait_ge(e_product, q + 1)
                        if s < STEPS - 1:
                            wait(dve, ztil, q + (UNITS - 1))
                        for g in range(G):
                            col = bass.ds(u * G + g, 1)
                            if s in NORM_L:
                                ins = nc.vector.scalar_tensor_tensor(
                                    out=UB[p][:, g, :], in0=MB2[p][:, g, :], scalar=dinv[:, col],
                                    in1=(bf1_bc if s else b1_bc)[:, :], op0=ALU.mult, op1=ALU.add)
                            elif s < STEPS - 1:
                                if g == 0:
                                    dve.wait_ge(bi_in[p], (u - p) * 8 + 16 * (done_before(BI_L, s) + 1))
                                ins = nc.vector.scalar_tensor_tensor(
                                    out=ZN[p][:, g, :], in0=MB2[p][:, g, :], scalar=dinv[:, col],
                                    in1=BI[p][:, g, :], op0=ALU.mult, op1=ALU.add)
                            else:
                                if g == 0:
                                    dve.wait_ge(ax_in[p], (u - p) * 8 + 16 * (done_before(AX_L, s) + 1))
                                    wait(dve, scat[p], (u - p) * 16)
                                ins = nc.vector.scalar_tensor_tensor(
                                    out=Y2[p][:, g, :], in0=MB2[p][:, g, 0:D], scalar=dinv_half[:, col],
                                    in1=RI[p][:, g, :], op0=ALU.mult, op1=ALU.add)
                        ins.then_inc(e_early, 1)

                    def clamp(u, p):
                        if s in NORM_L:
                            dve.wait_ge(e_squared, u + (NORM_L.index(s) * UNITS + 1))
                            nc.vector.tensor_scalar(ecl[p][:, :], en2[p][:, :], EPS_NORM ** 2,
                                                    COEF.get(s, 1.0) ** -2, ALU.max, ALU.mult).then_inc(e_clamped, 1)
                        elif s == STEPS - 1:
                            dve.wait_ge(e_early, u + (s * UNITS + 1))
                            for g in range(G):
                                ins = nc.vector.bn_stats(est[p][:, g, :], Y2[p][:, g, :])
                            ins.then_inc(e_own, 1)
                            wait_apart(dve, e_own, u * 3 + 1)
                            for g in range(G):
                                ins = nc.vector.bn_aggr(emv[p][:, g, :], est[p][:, g, :])
                            ins.then_inc(e_own, 1)
                            dve.wait_ge(e_own, u * 3 + 2)
                            nc.vector.tensor_scalar_add(ecl[p][:, :], emv[p][:, :, 1], EPS_LN).then_inc(e_clamped, 1)

                    def late(u, p):
                        if s in NORM_L:
                            n = NORM_L.index(s) * UNITS
                            dve.wait_ge(e_root, u + (n + 1))
                            nc.vector.reciprocal(eS[p][:, :], ert[p][:, :]).then_inc(e_recip, 1)
                            dve.wait_ge(e_recip, u + (n + 1))
                            if s:
                                nc.vector.tensor_tensor(eSD[p][:, :], eS[p][:, :], dinv[:, bass.ds(u * G, G)],
                                                        ALU.mult).then_inc(e_scale, 1)
                            else:
                                for g in range(G):
                                    ins = nc.vector.tensor_scalar(ZN[p][:, g, :], UB[p][:, g, :], eS[p][:, g:g + 1],
                                                                  None, ALU.mult)
                                ins.then_inc(e_scale, 1)
                        if s in RK_L:
                            n = RK_L.index(s) * UNITS
                            wait(dve, bo_out[p], (u - p) * 8 + 16 * done_before(BO_L, s))
                            if s in XO_L:
                                wait(dve, xo_out[p], (u - p) * 8 + 16 * done_before(XO_L, s))
                            if s in (2, 4, 6):
                                dve.wait_ge(e_early, u + (s * UNITS + 1))
                                dve.wait_ge(ax_in[p], (u - p) * 8 + 16 * (done_before(AX_L, s) + 1))
                            if s == 0:
                                dve.wait_ge(e_scale, u + 1)
                                nc.vector.tensor_tensor(XO[p][:, :, :], ZN[p][:, :, :],
                                                        bf2_half[:, :, :].to_broadcast([P, G, H]), ALU.add).then_inc(rk_step, 1)
                                dve.wait_ge(rk_step, u + 1)
                                nc.vector.scalar_tensor_tensor(out=BO[p][:, :, :], in0=ZN[p][:, :, :], scalar=0.5,
                                                               in1=XO[p][:, :, :], op0=ALU.mult, op1=ALU.add).then_inc(rk_done, 1)
                            elif s == 2:
                                nc.vector.scalar_tensor_tensor(out=BO[p][:, :, :], in0=ZN[p][:, :, :], scalar=0.5,
                                                               in1=AX_[p][:, :, :], op0=ALU.mult, op1=ALU.add).then_inc(rk_done, 1)
                            elif s == 4:
                                own = UNITS
                                nc.vector.tensor_tensor(XO[p][:, :, :], AX_[p][:, :, :],
                                                        bf2_half[:, :, :].to_broadcast([P, G, H]), ALU.add).then_inc(rk_step, 1)
                                dve.wait_ge(rk_step, u * 3 + (own + 1))
                                nc.vector.tensor_tensor(BO[p][:, :, :], ZN[p][:, :, :], XO[p][:, :, :], ALU.add).then_inc(rk_step, 1)
                                dve.wait_ge(rk_step, u * 3 + (own + 2))
                                nc.vector.tensor_tensor(XO[p][:, :, :], BI[p][:, :, :], BO[p][:, :, :], ALU.add).then_inc(rk_step, 1)
                                dve.wait_ge(rk_step, u * 3 + (own + 3))
                                nc.vector.scalar_tensor_tensor(out=XO[p][:, :, :], in0=AX_[p][:, :, :], scalar=-2.5,
                                                               in1=XO[p][:, :, :], op0=ALU.mult, op1=ALU.add).then_inc(rk_done, 1)
                            elif s == 6:
                                nc.vector.scalar_tensor_tensor(out=BO[p][:, :, :], in0=AX_[p][:, :, :], scalar=4.0 / 3.0,
                                                               in1=ZN[p][:, :, :], op0=ALU.mult, op1=ALU.add).then_inc(rk_done, 1)
                        if s == STEPS - 1:
                            dve.wait_ge(e_root, u + (len(NORM_L) * UNITS + 1))
                            nc.vector.reciprocal(eS[p][:, :], ert[p][:, :]).then_inc(e_own, 1)
                            dve.wait_ge(e_own, u * 3 + 3)
                            for g in range(G):
                                ins = nc.vector.tensor_scalar(Y2[p][:, g, :], Y2[p][:, g, :], emv[p][:, g, 0:1],
                                                              eS[p][:, g:g + 1], ALU.subtract, ALU.mult)
                            ins.then_inc(y2_done, 1)

                    def at(u, p, there):
                        o = 1 - p
                        if there(-1):
                            clamp(u - 1, o)
                        if there(1):
                            dve.wait_ge(e_high, u + (s * UNITS + 2))
                            nc.vector.tensor_tensor(EL[o][:, 0:nb], TB2[o][:, 0:nb], EH[o][:, 0:nb].bitcast(fp32),
                                                    ALU.subtract).then_inc(e_low, 1)
                        if there(3):
                            matrices(u + 3, o)
                            source_low(u + 3, o)
                        if there(2):
                            add_own(u + 2, p)
                        if there(-1):
                            late(u - 1, o)
                        if there(0):
                            early(u, p)

                    positions(dve, at)


_INS = ['x', 'src_pad', 'dst_pad', 'W1', 'b1', 'Wf1', 'bf1', 'Wf2', 'bf2', 'W2', 'b2']
_OUTS = [((50000, 128), 'float32')]


def kernel(**inputs):
    import numpy as _np
    import concourse.bacc as _bacc
    from concourse import mybir as _mybir
    from concourse.bass_utils import run_bass_kernel_spmd as _run

    named = {n.removeprefix('L0_gnn_'): _np.asarray(a) for n, a in inputs.items()}
    edges, nodes = named['src'].shape[0], named['x'].shape[0]
    padded = -(-edges // 512) * 512
    named['src_pad'] = _np.concatenate([named.pop('src'), _np.zeros(padded - edges, _np.int32)])
    named['dst_pad'] = _np.concatenate([_np.full(1, -1, _np.int32), named.pop('dst'),
                                        _np.full(padded - edges, nodes, _np.int32), _np.full(1, -1, _np.int32)])
    nc = _bacc.Bacc("TRN2", target_bir_lowering=False, num_devices=1)
    arrays, args = {}, []
    for name in _INS:
        a = _np.ascontiguousarray(named[name])
        arrays[f"in_{name}_dram"] = a
        args.append(nc.dram_tensor(f"in_{name}_dram", a.shape, _mybir.dt.from_np(a.dtype), kind="ExternalInput").ap())
    for i, (shape, dtype) in enumerate(_OUTS):
        dt = _mybir.dt.from_np(_np.dtype(dtype))
        args.append(nc.dram_tensor(f"out_{i}_dram", shape, dt, kind="ExternalOutput").ap())
    bass_gnn_rk4_resnorm(nc, *args)
    r = _run(nc, [arrays], core_ids=[0])
    return r.results[0]["out_0_dram"]
```

```python
import concourse.bass as bass
from concourse import mybir
from contextlib import ExitStack


def bass_gnn_rk4_resnorm(
    nc: bass.Bass,
    x: bass.AP,
    src_pad: bass.AP,
    dst_pad: bass.AP,
    W1: bass.AP,
    b1: bass.AP,
    Wf1: bass.AP,
    bf1: bass.AP,
    Wf2: bass.AP,
    bf2: bass.AP,
    W2: bass.AP,
    b2: bass.AP,
    out: bass.AP,
):
    fp32 = mybir.dt.float32
    fp32r = mybir.dt.float32r
    bf16 = mybir.dt.bfloat16
    i32 = mybir.dt.int32
    ALU = mybir.AluOpType
    ACT = mybir.ActivationFunctionType
    AX = mybir.AxisListType

    P = 128
    N, D = x.shape
    H = W1.shape[1]
    KB = H // P
    RING = 4
    G = 2
    LANES = 4
    ROWS = LANES * G * P
    ITERS = -(-N // ROWS)
    LAST_BASE = N - ROWS
    STEPS = 10
    SLOTS = STEPS * LANES
    LAG = 2
    OFF = (0, 1, 3, 4)
    EPS_NORM = 1e-12
    EPS_LN = 1e-5

    E_PAD = dst_pad.shape[0] - 2
    ET = E_PAD // P
    UNITS = ET // G
    SLOT_ROW0 = N
    N_PAD = -(-N // P) * P
    T_ROWS = SLOT_ROW0 + E_PAD
    SKIP = 1 << 20
    CHUNK = next(c for c in range(1, ET + 1) if ET % c == 0 and 2 * (ET // c) <= ITERS - 2)
    SWEEP = ET // CHUNK

    COEF = {1: 0.5, 3: 0.5, 5: 1.0, 7: 1.0 / 3.0}
    NORM_STEPS = [0, 1, 3, 5, 7]
    Z_STEPS = [0, 2, 4, 6, 8]
    F1_STEPS = [1, 3, 5, 7]

    tables = [nc.dram_tensor(f"table{s}", (T_ROWS, D if s == 0 else H), fp32).ap() for s in range(STEPS)]
    node_row = nc.dram_tensor("node_row", (N_PAD, 1), i32).ap()
    seg_dram = nc.dram_tensor("seg_dram", (ET, P), bf16).ap()
    resid_dram = nc.dram_tensor("resid_dram", (E_PAD, D), fp32).ap()
    xb_dram = nc.dram_tensor("xb_dram", (E_PAD, H), fp32).ap()
    base_dram = [nc.dram_tensor(f"base_dram{n}", (E_PAD, H), fp32).ap() for n in range(2)]
    q_dram = nc.dram_tensor("q_dram", (E_PAD, H), fp32).ap()

    ctx = ExitStack()
    with ctx:
        def sb(name, shape, dt, c=ctx):
            return c.enter_context(nc.sbuf_tensor(name, shape, dt))

        def pb(name, shape, dt, c=ctx):
            return c.enter_context(nc.psum_tensor(name, shape, dt))

        def sem(name, c=ctx):
            return c.enter_context(nc.semaphore(name))

        w1 = [sb(f"w1_{p}", [P, 1, H], fp32r) for p in ("hi", "lo")]
        wf1 = [sb(f"wf1_{p}", [P, KB, H], fp32r) for p in ("hi", "lo")]
        wf2 = [sb(f"wf2_{p}", [P, KB, H], fp32r) for p in ("hi", "lo")]
        w2_parts = sb("w2_parts", [P, KB, 2, D], fp32r)
        w2 = [w2_parts[:, :, part, :] for part in range(2)]
        ident = sb("ident", [P, P], fp32)
        bias_rows = sb("bias_rows", [64, 2, H], fp32r)
        ones_rows = sb("ones_rows", [64, P], fp32r)
        bf2_half = sb("bf2_half", [P, 1, H], fp32)
        b1_bc = sb("b1_bc", [P, H], fp32)
        bf1_bc = sb("bf1_bc", [P, H], fp32)
        b2_bc = sb("b2_bc", [P, 1, D], fp32)
        dinv = sb("dinv", [P, ET], fp32)
        dinv_half = sb("dinv_half", [P, ET], fp32)
        seg_col = sb("seg_col", [P, ET], fp32)
        src_row = sb("src_row", [P, ET], i32)
        self_idx = sb("self_idx", [P, ET], i32)
        out_idx = sb("out_idx", [P, ET], i32)
        src_idx = sb("src_idx", [P, ET], i32)
        slot_row = sb("slot_row", [P, ET], i32)

        weights = {0: w1, STEPS - 1: w2}
        for s in range(1, STEPS - 1):
            weights[s] = wf1 if s % 2 else wf2

        def last_product(out_, high_, low_):
            for m, (of, b) in enumerate(((high_, 0), (low_, 0), (low_, 1), (high_, 1))):
                n = 2 if of is high_ else 1
                mm = nc.tensor.matmul(out_[:, 0:n * D], of(b), w2_parts[:, b, 0:n, :].rearrange("p n d -> p (n d)"),
                                      start=m == 0, stop=m == 3)
            return mm

        def transpose(out_, in_):
            return nc.tensor.transpose(out_, in_, ident[:, :])

        waited = sem("waited")

        with ExitStack() as c:
            w_raw = sb("w_raw", [P, 3 * KB * H], fp32, c)
            raw = {"w1": w_raw[:, 0:H].rearrange("p (b n) -> p b n", b=1)}
            at = H
            for name, n in (("wf1", H), ("wf2", H), ("w2", D)):
                raw[name] = w_raw[:, at:at + KB * n].rearrange("p (b n) -> p b n", b=KB)
                at += KB * n
            b_raw = sb("b_raw", [64, 2, H], fp32, c)
            bf2_bc = sb("bf2_bc", [P, H], fp32, c)
            dsti = sb("dsti", [ET, 3, P], i32, c)
            srci = sb("srci", [ET, P], i32, c)
            edge_no = sb("edge_no", [ET, P], fp32, c)
            dstf = sb("dstf", [ET, 3, P], fp32, c)
            first = sb("first", [ET, P], fp32, c)
            last = sb("last", [ET, P], fp32, c)
            zeros = sb("zeros", [ET, P], fp32, c)
            seg = sb("seg", [ET, P], fp32, c)
            start = sb("start", [ET, P], fp32, c)
            tail = sb("tail", [ET, ET], fp32, c)
            ones_t = sb("ones_t", [ET, ET], fp32, c)
            before = sb("before", [ET, ET], fp32, c)
            carry = sb("carry", [ET, 1], fp32, c)
            deg = sb("deg", [ET, P], fp32, c)
            rt = sb("rt", [ET, P], fp32, c)
            di = sb("di", [ET, P], fp32, c)
            tmp = sb("tmp", [ET, P], fp32, c)
            rows = sb("rows", [ET, 5, P], fp32, c)
            seg_bf = sb("seg_bf", [ET, P], bf16, c)
            node_no = sb("node_no", [P, N_PAD // P], i32, c)
            ps_tail = pb("ps_tail", [ET, ET], fp32, c)
            ps_rows = pb("ps_rows", [P, 5, P], fp32, c)

            w_in = sem("w_in", c)
            e_in = sem("e_in", c)
            iotas = sem("iotas", c)
            b_zero = sem("b_zero", c)
            v = sem("v", c)
            tail_sum = sem("tail_sum", c)
            rooted = sem("rooted", c)
            rows_t = sem("rows_t", c)
            cols_done = sem("cols_done", c)
            map_init = sem("map_init", c)
            map_out = sem("map_out", c)
            seg_out = sem("seg_out", c)

            block = c.enter_context(nc.Block())

            @block.sync
            def _(sp):
                sp.dma_start(dsti[:, 1, :], dst_pad[1:1 + E_PAD].rearrange("(t j) -> t j", j=P)).then_inc(e_in, 16)
                sp.dma_start(dsti[:, 0, :], dst_pad[0:E_PAD].rearrange("(t j) -> t j", j=P)).then_inc(e_in, 16)
                sp.dma_start(dsti[:, 2, :], dst_pad[2:2 + E_PAD].rearrange("(t j) -> t j", j=P)).then_inc(e_in, 16)
                sp.dma_start(srci[:, :], src_pad.rearrange("(t j) -> t j", j=P)).then_inc(e_in, 16)
                sp.dma_start(raw["w1"][:, 0, :], W1).then_inc(w_in, 16)
                sp.dma_start(raw["wf1"], Wf1.rearrange("(b p) n -> p b n", p=P)).then_inc(w_in, 16)
                sp.dma_start(raw["wf2"], Wf2.rearrange("(b p) n -> p b n", p=P)).then_inc(w_in, 16)
                sp.dma_start(raw["w2"], W2.rearrange("(b p) n -> p b n", p=P)).then_inc(w_in, 16)
                sp.wait_ge(b_zero, 1)
                for r in (0, 32):
                    sp.dma_start(b_raw[r:r + 1, 0, :], b1.rearrange("(a n) -> a n", a=1)).then_inc(w_in, 16)
                    sp.dma_start(b_raw[r:r + 1, 1, :], bf1.rearrange("(a n) -> a n", a=1)).then_inc(w_in, 16)
                for to, of in ((b1_bc[:, :], b1), (bf1_bc[:, :], bf1), (bf2_bc[:, :], bf2), (b2_bc[:, 0, :], b2)):
                    sp.dma_start(to, of.rearrange("(a n) -> a n", a=1).to_broadcast([P, of.shape[0]])).then_inc(w_in, 16)
                sp.wait_ge(map_init, 1)
                sp.dma_start(node_row.rearrange("(p c) a -> p (c a)", p=P), node_no[:, :]).then_inc(map_out, 16)
                sp.wait_ge(cols_done, 1)
                sp.dma_start(seg_dram, seg_bf[:, :]).then_inc(seg_out, 16)
                sp.wait_ge(seg_out, 16)
                sp.wait_ge(map_out, 16)

            @block.gpsimd
            def _(pool):
                pool.iota(edge_no[:, :], [[1, P]], base=0, channel_multiplier=P,
                          allow_small_or_imprecise_dtypes=True).then_inc(iotas, 1)
                pool.memset(zeros[:, :], 0.0).then_inc(iotas, 1)
                pool.memset(ones_t[:, :], 1.0).then_inc(iotas, 1)
                pool.memset(b_raw[:, :, :], 0.0).then_inc(b_zero, 1)
                pool.memset(ident[:, :], 0.0).then_inc(iotas, 1)
                pool.wait_ge(iotas, 4)
                pool.affine_select(out=ident[:, :], in_=ident[:, :], compare_op=ALU.not_equal, fill=1.0,
                                   base=0, pattern=[[-1, P]], channel_multiplier=1).then_inc(iotas, 1)
                pool.affine_select(out=before[:, :], in_=ones_t[:, :], compare_op=ALU.is_gt, fill=0.0,
                                   base=0, pattern=[[-1, ET]], channel_multiplier=1).then_inc(iotas, 1)
                pool.iota(slot_row[:, :], [[P, ET]], base=SLOT_ROW0, channel_multiplier=1).then_inc(iotas, 1)
                pool.iota(node_no[:, :], [[1, N_PAD // P]], base=0,
                          channel_multiplier=N_PAD // P).then_inc(map_init, 1)

            @block.vector
            def _(dve):
                steps = [0]

                def step(ins):
                    steps[0] += 1
                    ins.then_inc(v, 1)
                    dve.wait_ge(v, steps[0])

                dve.wait_ge(e_in, 64)
                dve.wait_ge(iotas, 7)
                step(nc.vector.tensor_copy(dstf[:, :, :], dsti[:, :, :]))
                step(nc.vector.tensor_tensor(first[:, :], dstf[:, 1, :], dstf[:, 0, :], ALU.not_equal))
                step(nc.vector.tensor_tensor(last[:, :], dstf[:, 1, :], dstf[:, 2, :], ALU.not_equal))
                step(nc.vector.tensor_tensor_scan(seg[:, :], first[:, :], zeros[:, :], 0.0, ALU.add, ALU.add))
                step(nc.vector.tensor_tensor(tmp[:, :], first[:, :], edge_no[:, :], ALU.mult))
                step(nc.vector.tensor_tensor_scan(start[:, :], tmp[:, :], zeros[:, :], 0.0, ALU.max, ALU.max))
                nc.vector.tensor_scalar(tail[:, :], ident[0:ET, 0:ET], start[:, P - 1:P], None,
                                        ALU.mult).then_inc(v, 1)
                steps[0] += 1
                dve.wait_ge(tail_sum, 1)
                step(nc.vector.tensor_tensor(tail[:, :], ps_tail[:, :], before[:, :], ALU.mult))
                step(nc.vector.tensor_reduce(carry[:, :], tail[:, :], AX.X, ALU.max))
                step(nc.vector.tensor_scalar(start[:, :], start[:, :], carry[:, 0:1], None, ALU.max))
                step(nc.vector.tensor_tensor(deg[:, :], edge_no[:, :], start[:, :], ALU.subtract))
                nc.vector.tensor_scalar_add(deg[:, :], deg[:, :], 2.0).then_inc(v, 1)
                steps[0] += 1
                dve.wait_ge(rooted, 1)
                step(nc.vector.reciprocal(di[:, :], rt[:, :]))
                step(nc.vector.tensor_tensor(tmp[:, :], di[:, :], di[:, :], ALU.mult))
                step(nc.vector.tensor_tensor(tmp[:, :], tmp[:, :], deg[:, :], ALU.mult))
                step(nc.vector.tensor_scalar(tmp[:, :], tmp[:, :], -0.5, 1.5, ALU.mult, ALU.add))
                step(nc.vector.tensor_tensor(di[:, :], di[:, :], tmp[:, :], ALU.mult))
                step(nc.vector.tensor_scalar(tmp[:, :], dstf[:, 1, :], float(N), None, ALU.is_lt))
                step(nc.vector.tensor_tensor(last[:, :], last[:, :], tmp[:, :], ALU.mult))
                step(nc.vector.tensor_scalar_add(tmp[:, :], dstf[:, 1, :], -float(SKIP)))
                step(nc.vector.tensor_tensor(tmp[:, :], tmp[:, :], last[:, :], ALU.mult))
                step(nc.vector.tensor_scalar_add(tmp[:, :], tmp[:, :], float(SKIP)))
                step(nc.vector.tensor_copy(dstf[:, 2, :], srci[:, :]))
                step(nc.vector.tensor_scalar(dstf[:, 0, :], dstf[:, 1, :], float(N - 1), None, ALU.min))
                for n, row in enumerate((di[:, :], seg[:, :], dstf[:, 2, :], dstf[:, 0, :], tmp[:, :])):
                    nc.vector.tensor_copy(rows[:, n, 1:P - 1], row[:, 1:P - 1])
                    nc.vector.tensor_copy(rows[:, n, 0:1], row[:, P - 1:P])
                    step(nc.vector.tensor_copy(rows[:, n, P - 1:P], row[:, 0:1]))
                nc.vector.tensor_copy(seg_bf[:, :], rows[:, 1, :]).then_inc(cols_done, 1)
                dve.wait_ge(rows_t, 1)
                nc.vector.tensor_copy(dinv[:, :], ps_rows[:, 0, 0:ET])
                nc.vector.tensor_scalar(dinv_half[:, :], ps_rows[:, 0, 0:ET], 0.5, None, ALU.mult)
                nc.vector.tensor_copy(seg_col[:, :], ps_rows[:, 1, 0:ET])
                nc.vector.tensor_copy(src_idx[:, :], ps_rows[:, 2, 0:ET])
                nc.vector.tensor_copy(self_idx[:, :], ps_rows[:, 3, 0:ET])
                nc.vector.tensor_copy(out_idx[:, :], ps_rows[:, 4, 0:ET]).then_inc(cols_done, 1)
                dve.wait_ge(w_in, 12 * 16)
                for name, (hi, lo) in (("w1", w1), ("wf1", wf1), ("wf2", wf2), ("w2", w2)):
                    hi, lo = hi[:, :, :], lo[:, :, :]
                    step(nc.vector.tensor_copy(hi, raw[name]))
                    step(nc.vector.tensor_tensor(lo, raw[name], hi.bitcast(fp32), ALU.subtract))
                step(nc.vector.tensor_copy(bias_rows[:, :, :], b_raw[:, :, :]))
                step(nc.vector.tensor_tensor(bias_rows[32:33, :, :], b_raw[32:33, :, :],
                                             bias_rows[32:33, :, :].bitcast(fp32), ALU.subtract))
                step(nc.vector.tensor_scalar(ones_rows[:, :], ident[0:64, :], 0.0, 1.0, ALU.mult, ALU.add))
                step(nc.vector.tensor_scalar(bf2_half[:, 0, :], bf2_bc[:, :], 0.5, None, ALU.mult))

            @block.scalar
            def _(act):
                act.wait_ge(v, 12)
                nc.scalar.activation(rt[:, :], deg[:, :], ACT.Sqrt).then_inc(rooted, 1)

            @block.tensor
            def _(pe):
                pe.wait_ge(v, 7)
                nc.tensor.matmul(ps_tail[:, :], ones_t[:, :], tail[:, :], start=True, stop=True).then_inc(tail_sum, 1)
                pe.wait_ge(cols_done, 1)
                for n in range(5):
                    mm = nc.tensor.transpose(ps_rows[:, n, 0:ET], rows[:, n, :], ident[0:ET, 0:ET])
                mm.then_inc(rows_t, 1)

        with ExitStack() as c:
            xt = sb("xt", [P, LANES, G, D], fp32, c)
            xres = sb("xres", [P, LANES, G, D], fp32, c)
            Z = [sb(f"Z{l}", [P, G, H], fp32, c) for l in range(LANES)]
            U = [sb(f"U{l}", [P, G, H], fp32, c) for l in range(LANES)]
            ZS = [sb(f"ZS{l}", [P, G, H], fp32, c) for l in range(LANES)]
            HI = [sb(f"HI{l}", [P, KB, G, P], fp32r, c) for l in range(LANES)]
            LO = [sb(f"LO{l}", [P, KB, G, P], fp32r, c) for l in range(LANES)]
            XB = [sb(f"XB{l}", [P, G, H], fp32, c) for l in range(LANES)]
            XQ = [sb(f"XQ{l}", [P, G, H], fp32, c) for l in range(LANES)]
            BA = [sb(f"BA{l}", [P, G, H], fp32, c) for l in range(LANES)]
            BB = [sb(f"BB{l}", [P, G, H], fp32, c) for l in range(LANES)]
            Y = [sb(f"Y{l}", [P, G, D], fp32, c) for l in range(LANES)]
            norm2 = [sb(f"norm2_{l}", [P, G], fp32, c) for l in range(LANES)]
            clamped = [sb(f"clamped{l}", [P, G], fp32, c) for l in range(LANES)]
            root = [sb(f"root{l}", [P, G], fp32, c) for l in range(LANES)]
            S = [sb(f"S{l}", [P, G], fp32, c) for l in range(LANES)]
            SL = [sb(f"SL{l}", [P, G], fp32, c) for l in range(LANES)]
            stats = [sb(f"stats{l}", [P, G, 6], fp32, c) for l in range(LANES)]
            mv = [sb(f"mv{l}", [P, G, 2], fp32, c) for l in range(LANES)]
            square = [sb(f"square{l}", [P, G, H], fp32, c) for l in range(LANES)]
            at_idx = sb("at_idx", [P, CHUNK], i32, c)
            own_idx = sb("own_idx", [P, CHUNK], i32, c)
            row_val = sb("row_val", [P, CHUNK], i32, c)
            slot_x = sb("slot_x", [P, CHUNK, D], fp32, c)
            slot_xs = sb("slot_xs", [P, CHUNK, D], fp32, c)
            slot_xr = sb("slot_xr", [P, CHUNK, D], fp32, c)
            TB = [pb(f"TB{l}", [P, KB, G, P], fp32, c) for l in range(LANES)]
            MB = [pb(f"MB{l}", [P, G, H], fp32, c) for l in range(LANES)]

            def lane_sems(name):
                return [sem(f"{name}{l}", c) for l in range(LANES)]

            x_in = lane_sems("x_in")
            xres_in = lane_sems("xres_in")
            t0_out = lane_sems("t0_out")
            z_out = lane_sems("z_out")
            zs_out = lane_sems("zs_out")
            y_out = lane_sems("y_out")
            transposed = lane_sems("transposed")
            product = lane_sems("product")
            high = lane_sems("high")
            low = lane_sems("low")
            u_done = lane_sems("u_done")
            squared = lane_sems("squared")
            clamp_done = lane_sems("clamp_done")
            var_done = lane_sems("var_done")
            root_done = lane_sems("root_done")
            s_done = lane_sems("s_done")
            z_done = lane_sems("z_done")
            zs_done = lane_sems("zs_done")
            sum_done = lane_sems("sum_done")
            base_done = lane_sems("base_done")
            y_sum = lane_sems("y_sum")
            stats_done = lane_sems("stats_done")
            y_done = lane_sems("y_done")
            staged = sem("staged", c)
            scattered = sem("scattered", c)
            slot_x_in = sem("slot_x_in", c)
            slot_scaled = sem("slot_scaled", c)
            slot_out = sem("slot_out", c)
            row_in = sem("row_in", c)
            row_taken = sem("row_taken", c)

            block = c.enter_context(nc.Block())

            NZ, NF, NN = len(Z_STEPS), len(F1_STEPS), len(NORM_STEPS)
            SUM = {"x1+bf2/2": 1, "x1+bf2": 2, "q": 3, "x+b2": 4}
            BASE = {"2nd": 1, "3rd": 2, "4th": 3, "last's first part": 4, "last": 5}
            NR = NN + 1
            ORDER = [((j - OFF[l]) % STEPS, l, int(j < OFF[l])) for j in range(STEPS) for l in range(LANES)]

            def waits_for_first(k):
                return ORDER[k % SLOTS][0] == 1

            def slot(i, k):
                ahead, k = divmod(k, SLOTS)
                s, l, earlier = ORDER[k]
                n = (i, ahead - earlier)
                if isinstance(i, int):
                    n = (i + ahead - earlier, 0)
                    if not 0 <= n[0] < ITERS:
                        return None
                return s, l, n

            def count(n, per_pass, m):
                i, distance = n
                return i * per_pass + (distance * per_pass + m)

            def wait(eng, s_, value):
                if not isinstance(value, int) or value > 0:
                    eng.wait_ge(s_, value)

            def passes(eng, position, unrolled_end=2):
                def iteration(i):
                    for k in range(SLOTS):
                        position(i, k)

                iteration(0)
                iteration(1)
                with eng.Fori(2, ITERS + 1 - unrolled_end) as i:
                    iteration(i)
                for i in range(ITERS + 1 - unrolled_end, ITERS + 1):
                    iteration(i)

            def by_row(table, n, l):
                base = min(n[0] * ROWS, LAST_BASE) if isinstance(n[0], int) else count(n, ROWS, 0)
                return table[bass.ds(base, ROWS), :].rearrange("(p l g) f -> p l g f", p=P, l=LANES)[:, l]

            assert N % (LANES * G) == 0

            @block.sync
            def _(sp):
                def store(table, n, l, of, done, per_pass, m):
                    if isinstance(n[0], int) and n[0] == ITERS - 1:
                        wait(sp, done[l], 16 * count(n, per_pass, m))
                    sp.dma_start(by_row(table, n, l), of).then_inc(done[l], 16)

                def position(i, k):
                    if slot(i, k) is None:
                        return
                    s, l, n = slot(i, k)
                    if s == 0:
                        sp.wait_ge(x_in[l], count(n, 16, 16))
                        store(tables[0], n, l, xt[:, l], t0_out, 1, 0)
                    if s in Z_STEPS:
                        sp.wait_ge(z_done[l], count(n, NZ, Z_STEPS.index(s) + 1))
                        store(tables[s + 1], n, l, Z[l][:, :, :], z_out, NZ, Z_STEPS.index(s))
                    elif s in F1_STEPS:
                        sp.wait_ge(zs_done[l], count(n, NF, F1_STEPS.index(s) + 1))
                        store(tables[s + 1], n, l, ZS[l][:, :, :], zs_out, NF, F1_STEPS.index(s))
                    else:
                        sp.wait_ge(y_done[l], count(n, 1, 1))
                        store(out, n, l, Y[l][:, :, :], y_out, 1, 0)
                    if s == 1:
                        wait(sp, y_sum[l], count(n, 1, 0))
                        sp.dma_start(xres[:, l], by_row(x, n, l)).then_inc(xres_in[l], 16)
                        following = (n[0], n[1] + 1) if not isinstance(n[0], int) else (n[0] + 1, 0)
                        if not isinstance(n[0], int) or following[0] < ITERS:
                            sp.wait_ge(t0_out[l], count(n, 16, 16))
                            sp.wait_ge(transposed[l], count(n, STEPS, 1))
                            sp.dma_start(xt[:, l], by_row(x, following, l)).then_inc(x_in[l], 16)

                for l in range(LANES):
                    sp.dma_start(xt[:, l], by_row(x, (0, 0), l)).then_inc(x_in[l], 16)
                passes(sp, position, 3)
                for l in range(LANES):
                    sp.wait_ge(t0_out[l], 16 * ITERS)
                    sp.wait_ge(z_out[l], 16 * ITERS * NZ)
                    sp.wait_ge(zs_out[l], 16 * ITERS * NF)
                    sp.wait_ge(y_out[l], 16 * ITERS)

            @block.tensor
            def _(pe):
                def transposes(i, k):
                    if slot(i, k) is None:
                        return
                    s, l, n = slot(i, k)
                    if s == 0:
                        pe.wait_ge(x_in[l], count(n, 16, 16))
                    elif s - 1 in Z_STEPS:
                        pe.wait_ge(z_done[l], count(n, NZ, Z_STEPS.index(s - 1) + 1))
                    else:
                        pe.wait_ge(u_done[l], count(n, NF, F1_STEPS.index(s - 1) + 1))
                    of = xt[:, l] if s == 0 else Z[l] if s - 1 in Z_STEPS else U[l]
                    for g in range(G):
                        for b in range(1 if s == 0 else KB):
                            mm = transpose(TB[l][:, b, g, :], of[:, g, b * P:(b + 1) * P])
                    mm.then_inc(transposed[l], 1)

                def products(i, k):
                    if slot(i, k) is None:
                        return
                    s, l, n = slot(i, k)
                    if s == 0:
                        wait(pe, y_sum[l], count(n, 1, 0))
                    elif s - 1 in F1_STEPS:
                        pe.wait_ge(squared[l], count(n, NN, NORM_STEPS.index(s - 1) + 1))
                    pe.wait_ge(low[l], count(n, STEPS, s + 1))
                    hi, lo = weights[s]
                    w = D if s == STEPS - 1 else H
                    for g in range(G):
                        if s in NORM_STEPS:
                            nc.tensor.matmul(MB[l][:, g, 0:w], ones_rows[:, :], bias_rows[:, min(s, 1), :],
                                             start=True, stop=False)
                        terms = [(a, w_, b) for b in range(1 if s == 0 else KB)
                                 for a, w_ in ((LO[l], hi), (HI[l], lo), (HI[l], hi))]
                        for m, (a, w_, b) in enumerate(terms):
                            mm = nc.tensor.matmul(MB[l][:, g, 0:w], a[:, b, g, :], w_[:, b, :],
                                                  start=(m == 0 and s not in NORM_STEPS),
                                                  stop=(m == len(terms) - 1))
                    mm.then_inc(product[l], 1)

                def position(i, k):
                    if isinstance(i, int) and (i, k) == (0, 0):
                        for ahead in range(LAG):
                            transposes(0, ahead)
                    if not waits_for_first(k + LAG):
                        transposes(i, k + LAG)
                    products(i, k)
                    if waits_for_first(k + LAG):
                        transposes(i, k + LAG)

                passes(pe, position)

            @block.scalar
            def _(act):
                def high_part(i, k):
                    if slot(i, k) is None:
                        return
                    s, l, n = slot(i, k)
                    nb = 1 if s == 0 else KB
                    act.wait_ge(transposed[l], count(n, STEPS, s + 1))
                    nc.scalar.copy(HI[l][:, 0:nb], TB[l][:, 0:nb]).then_inc(high[l], 1)

                def squares(i, k):
                    if slot(i, k) is None:
                        return
                    s, l, n = slot(i, k)
                    if s in NORM_STEPS:
                        act.wait_ge(product[l], count(n, STEPS, s + 1))
                        if s in F1_STEPS:
                            wait(act, zs_done[l], count(n, NF, F1_STEPS.index(s)))
                            nc.scalar.copy(U[l][:, :, :], MB[l][:, :, :]).then_inc(u_done[l], 1)
                        for g in range(G):
                            sq = nc.scalar.activation(square[l][:, g, :], MB[l][:, g, :], ACT.Square,
                                                      accum_out=norm2[l][:, g:g + 1])
                        sq.then_inc(squared[l], 1)
                        act.wait_ge(squared[l], count(n, NN, NORM_STEPS.index(s) + 1))
                        nc.scalar.activation(root[l][:, :], norm2[l][:, :], ACT.Sqrt).then_inc(root_done[l], 1)

                def deviation(i, k):
                    if slot(i, k) is None:
                        return
                    s, l, n = slot(i, k)
                    if s == STEPS - 1:
                        act.wait_ge(var_done[l], count(n, 1, 1))
                        nc.scalar.activation(root[l][:, :], clamped[l][:, :], ACT.Sqrt).then_inc(root_done[l], 1)

                def position(i, k):
                    if isinstance(i, int) and (i, k) == (0, 0):
                        for ahead in range(LAG):
                            high_part(0, ahead)
                    if not waits_for_first(k + LAG):
                        high_part(i, k + LAG)
                    squares(i, k)
                    if waits_for_first(k + LAG):
                        high_part(i, k + LAG)
                    deviation(i, k - 1)

                passes(act, position)

            @block.vector
            def _(dve):
                def low_part(i, k):
                    if slot(i, k) is None:
                        return
                    s, l, n = slot(i, k)
                    nb = 1 if s == 0 else KB
                    dve.wait_ge(high[l], count(n, STEPS, s + 1))
                    nc.vector.tensor_tensor(LO[l][:, 0:nb], TB[l][:, 0:nb], HI[l][:, 0:nb].bitcast(fp32),
                                            ALU.subtract).then_inc(low[l], 1)

                def early(i, k):
                    if slot(i, k) is None:
                        return
                    s, l, n = slot(i, k)
                    if s in Z_STEPS and s > 0:
                        dve.wait_ge(product[l], count(n, STEPS, s + 1))
                        dve.wait_ge(z_out[l], count(n, 16 * NZ, 16 * Z_STEPS.index(s)))
                        dve.wait_ge(s_done[l], count(n, NN, NORM_STEPS.index(s - 1) + 1))
                        dve.wait_ge(base_done[l], count(n, 5, BASE[{2: "2nd", 4: "3rd", 6: "4th", 8: "last"}[s]]))
                        base = {2: BA, 4: BB, 6: BA, 8: BB}[s][l]
                        for g in range(G):
                            ins = nc.vector.scalar_tensor_tensor(
                                out=Z[l][:, g, :], in0=MB[l][:, g, :], scalar=S[l][:, g:g + 1], in1=base[:, g, :],
                                op0=ALU.mult, op1=ALU.add)
                        ins.then_inc(z_done[l], 1)
                    elif s == STEPS - 1:
                        dve.wait_ge(product[l], count(n, STEPS, s + 1))
                        dve.wait_ge(sum_done[l], count(n, 4, SUM["x+b2"]))
                        wait(dve, y_out[l], count(n, 16, 0))
                        nc.vector.scalar_tensor_tensor(out=Y[l][:, :, :], in0=MB[l][:, :, 0:D], scalar=0.5,
                                                       in1=xres[:, l], op0=ALU.mult, op1=ALU.add).then_inc(y_sum[l], 1)

                def bases(i, k):
                    if slot(i, k) is None:
                        return
                    s, l, n = slot(i, k)
                    if s == 1:
                        dve.wait_ge(sum_done[l], count(n, 4, SUM["x1+bf2/2"]))
                        nc.vector.scalar_tensor_tensor(out=BA[l][:, :, :], in0=Z[l][:, :, :], scalar=0.5,
                                                       in1=XB[l][:, :, :], op0=ALU.mult, op1=ALU.add).then_inc(base_done[l], 1)
                    elif s == 3:
                        dve.wait_ge(z_done[l], count(n, NZ, 2))
                        nc.vector.scalar_tensor_tensor(out=BB[l][:, :, :], in0=Z[l][:, :, :], scalar=0.5,
                                                       in1=XB[l][:, :, :], op0=ALU.mult, op1=ALU.add).then_inc(base_done[l], 1)
                    elif s == 5:
                        dve.wait_ge(z_done[l], count(n, NZ, 3))
                        dve.wait_ge(sum_done[l], count(n, 4, SUM["x1+bf2"]))
                        nc.vector.tensor_tensor(BA[l][:, :, :], Z[l][:, :, :], XQ[l][:, :, :],
                                                ALU.add).then_inc(base_done[l], 1)
                    elif s == 7:
                        dve.wait_ge(z_done[l], count(n, NZ, 4))
                        dve.wait_ge(sum_done[l], count(n, 4, SUM["q"]))
                        nc.vector.scalar_tensor_tensor(out=BA[l][:, :, :], in0=XQ[l][:, :, :], scalar=4.0 / 3.0,
                                                       in1=Z[l][:, :, :], op0=ALU.mult, op1=ALU.add).then_inc(base_done[l], 1)

                def variance(i, k):
                    if slot(i, k) is None:
                        return
                    s, l, n = slot(i, k)
                    if s == STEPS - 1:
                        dve.wait_ge(y_sum[l], count(n, 1, 1))
                        for g in range(G):
                            ins = nc.vector.bn_stats(stats[l][:, g, :], Y[l][:, g, :])
                        ins.then_inc(stats_done[l], 1)
                        dve.wait_ge(stats_done[l], count(n, 3, 1))
                        dve.sem_inc(waited, 1)
                        for g in range(G):
                            ins = nc.vector.bn_aggr(mv[l][:, g, :], stats[l][:, g, :])
                        ins.then_inc(stats_done[l], 1)
                        dve.wait_ge(stats_done[l], count(n, 3, 2))
                        nc.vector.tensor_scalar_add(clamped[l][:, :], mv[l][:, :, 1], EPS_LN).then_inc(var_done[l], 1)

                def scale(i, k):
                    if slot(i, k) is None:
                        return
                    s, l, n = slot(i, k)
                    if s not in NORM_STEPS:
                        return
                    m = NORM_STEPS.index(s)
                    dve.wait_ge(root_done[l], count(n, NR, m + 1))
                    nc.vector.tensor_scalar(clamped[l][:, :], root[l][:, :], EPS_NORM, 1.0 / COEF.get(s, 1.0),
                                            ALU.max, ALU.mult).then_inc(clamp_done[l], 1)
                    dve.wait_ge(clamp_done[l], count(n, NN, m + 1))
                    wait(dve, zs_done[l], count(n, NF, F1_STEPS.index(max(s, 1))))
                    nc.vector.reciprocal(S[l][:, :], clamped[l][:, :]).then_inc(s_done[l], 1)
                    if s == 0:
                        dve.wait_ge(s_done[l], count(n, NN, 1))
                        wait(dve, z_out[l], count(n, 16 * NZ, 0))
                        for g in range(G):
                            ins = nc.vector.tensor_scalar(Z[l][:, g, :], MB[l][:, g, :], S[l][:, g:g + 1], None, ALU.mult)
                        ins.then_inc(z_done[l], 1)

                def normalised(i, k):
                    if slot(i, k) is None:
                        return
                    s, l, n = slot(i, k)
                    if s == 7:
                        dve.wait_ge(base_done[l], count(n, 5, BASE["last's first part"]))
                        nc.vector.scalar_tensor_tensor(out=BB[l][:, :, :], in0=XB[l][:, :, :], scalar=-10.0 / 3.0,
                                                       in1=BA[l][:, :, :], op0=ALU.mult, op1=ALU.add).then_inc(base_done[l], 1)
                    if s == STEPS - 1:
                        dve.wait_ge(root_done[l], count(n, NR, NR))
                        nc.vector.reciprocal(SL[l][:, :], root[l][:, :]).then_inc(stats_done[l], 1)
                        dve.wait_ge(stats_done[l], count(n, 3, 3))
                        for g in range(G):
                            ins = nc.vector.tensor_scalar(Y[l][:, g, :], Y[l][:, g, :], mv[l][:, g, 0:1], SL[l][:, g:g + 1],
                                                          ALU.subtract, ALU.mult)
                        ins.then_inc(y_done[l], 1)

                def position(i, k):
                    if isinstance(i, int) and (i, k) == (0, 0):
                        for ahead in range(LAG):
                            low_part(0, ahead)
                    if not waits_for_first(k + LAG):
                        low_part(i, k + LAG)
                    early(i, k)
                    scale(i, k)
                    if waits_for_first(k + LAG):
                        low_part(i, k + LAG)
                    bases(i, k)
                    variance(i, k)
                    normalised(i, k - 1)

                passes(dve, position)

            @block.gpsimd
            def _(pool):
                def position(i, k):
                    if slot(i, k) is None:
                        return
                    s, l, n = slot(i, k)
                    if s == 0:
                        pool.wait_ge(z_done[l], count(n, NZ, 1))
                        nc.gpsimd.tensor_tensor(XB[l][:, :, :], Z[l][:, :, :],
                                                bf2_half[:, :, :].to_broadcast([P, G, H]), ALU.add).then_inc(sum_done[l], 1)
                        pool.wait_ge(sum_done[l], count(n, 4, SUM["x1+bf2/2"]))
                        nc.gpsimd.tensor_tensor(XQ[l][:, :, :], XB[l][:, :, :],
                                                bf2_half[:, :, :].to_broadcast([P, G, H]), ALU.add).then_inc(sum_done[l], 1)
                    elif s in F1_STEPS:
                        m = F1_STEPS.index(s)
                        pool.wait_ge(u_done[l], count(n, NF, m + 1))
                        pool.wait_ge(s_done[l], count(n, NN, NORM_STEPS.index(s) + 1))
                        wait(pool, zs_out[l], count(n, 16 * NF, 16 * m))
                        nc.gpsimd.tensor_tensor(ZS[l][:, :, :], U[l][:, :, :],
                                                S[l][:, :].unsqueeze(2).to_broadcast([P, G, H]),
                                                ALU.mult).then_inc(zs_done[l], 1)
                        if s == 5:
                            pool.wait_ge(base_done[l], count(n, 5, BASE["4th"]))
                            nc.gpsimd.tensor_tensor(XQ[l][:, :, :], BA[l][:, :, :], BB[l][:, :, :],
                                                    ALU.add).then_inc(sum_done[l], 1)
                    elif s == 6:
                        pool.wait_ge(xres_in[l], count(n, 16, 16))
                        nc.gpsimd.tensor_tensor(xres[:, l], xres[:, l], b2_bc[:, :, :].to_broadcast([P, G, D]),
                                                ALU.add).then_inc(sum_done[l], 1)

                def set_rows(i, k):
                    at = bass.ds(i * CHUNK - CHUNK, CHUNK)
                    if k == 0:
                        wait(pool, scattered, i * (16 * CHUNK) - 16 * CHUNK)
                        pool.sem_inc(waited, 1)
                        nc.gpsimd.tensor_copy(at_idx[:, :], out_idx[:, at]).then_inc(staged, 1)
                        nc.gpsimd.tensor_copy(row_val[:, :], slot_row[:, at]).then_inc(staged, 1)
                        nc.gpsimd.tensor_copy(own_idx[:, :], self_idx[:, at]).then_inc(staged, 1)
                    elif k % 3 == 0 and k // 3 <= CHUNK:
                        n = k // 3 - 1
                        if n == 0:
                            pool.wait_ge(staged, i * 3)
                            pool.sem_inc(waited, 1)
                        pool.indirect_dma_start(
                            out=node_row, out_offset=bass.IndirectOffsetOnAxis(ap=at_idx[:, n:n + 1], axis=0),
                            in_=row_val[:, n:n + 1], in_offset=None,
                            bounds_check=N_PAD - 1, oob_is_err=False).then_inc(scattered, 16)
                        pool.indirect_dma_start(
                            out=slot_x[:, n, :], out_offset=None,
                            in_=x, in_offset=bass.IndirectOffsetOnAxis(ap=own_idx[:, n:n + 1], axis=0)).then_inc(slot_x_in, 16)
                    elif k == SLOTS - 1:
                        pool.wait_ge(slot_x_in, i * (16 * CHUNK))
                        pool.sem_inc(waited, 1)
                        wait(pool, slot_out, i * 32 - 32)
                        pool.sem_inc(waited, 1)
                        nc.gpsimd.tensor_tensor(slot_xs[:, :, :], slot_x[:, :, :],
                                                dinv[:, at].unsqueeze(2).to_broadcast([P, CHUNK, D]), ALU.mult).then_inc(slot_scaled, 1)
                        nc.gpsimd.tensor_tensor(slot_xr[:, :, :], slot_x[:, :, :],
                                                b2_bc[:, :, :].to_broadcast([P, CHUNK, D]), ALU.add).then_inc(slot_scaled, 1)
                        pool.wait_ge(slot_scaled, i * 2)
                        pool.sem_inc(waited, 1)
                        for table, first, of in ((tables[0], SLOT_ROW0, slot_xs), (resid_dram, 0, slot_xr)):
                            rows_ = table[bass.ds(i * (CHUNK * P) + (first - CHUNK * P), CHUNK * P), :]
                            pool.dma_start(rows_.rearrange("(t p) f -> p t f", p=P), of[:, :, :]).then_inc(slot_out, 16)

                def get_rows(i, k):
                    at = bass.ds(i * CHUNK - (CHUNK + ET), CHUNK)
                    if k == 0:
                        nc.gpsimd.tensor_copy(at_idx[:, :], src_idx[:, at]).then_inc(staged, 1)
                    elif k % 3 == 0 and k // 3 <= CHUNK:
                        n = k // 3 - 1
                        if n == 0:
                            pool.wait_ge(staged, i + 2 * SWEEP)
                            pool.sem_inc(waited, 1)
                        pool.indirect_dma_start(
                            out=row_val[:, n:n + 1], out_offset=None, in_=node_row,
                            in_offset=bass.IndirectOffsetOnAxis(ap=at_idx[:, n:n + 1], axis=0)).then_inc(row_in, 16)
                    elif k == SLOTS - 1:
                        pool.wait_ge(row_in, i * (16 * CHUNK) - 16 * ET)
                        pool.sem_inc(waited, 1)
                        nc.gpsimd.tensor_copy(src_row[:, at], row_val[:, :]).then_inc(row_taken, 1)
                        pool.wait_ge(row_taken, i - SWEEP)
                        pool.sem_inc(waited, 1)

                def iteration(i, extra=None):
                    for k in range(SLOTS):
                        if extra:
                            extra(i, k)
                        position(i, k)

                iteration(0)
                iteration(1, set_rows)
                with pool.Fori(2, 1 + SWEEP) as i:
                    iteration(i, set_rows)
                pool.wait_ge(scattered, 16 * ET)
                pool.wait_ge(slot_out, 32 * SWEEP)
                with pool.Fori(1 + SWEEP, 1 + 2 * SWEEP) as i:
                    iteration(i, get_rows)
                if 1 + 2 * SWEEP < ITERS - 1:
                    with pool.Fori(1 + 2 * SWEEP, ITERS - 1) as i:
                        iteration(i)
                iteration(ITERS - 1)
                iteration(ITERS)

        with ExitStack() as c:
            ZT = sb("ZT", [P, ET, H], fp32, c)
            seg_bc = sb("seg_bc", [P, ET * P], bf16, c)
            CR = [sb(f"CR{g}", [1, H], fp32, c) for g in range(G)]
            idx = [sb(f"idx{r}", [P, G], i32, c) for r in range(RING)]
            oidx = [sb(f"oidx{p}", [P, G], i32, c) for p in range(2)]
            GA = [sb(f"GA{r}", [P, G, H], fp32, c) for r in range(RING)]
            SM = [sb(f"SM{p}", [P, G, P], fp32, c) for p in range(2)]
            M0 = [sb(f"M0_{p}", [1, G, P], fp32, c) for p in range(2)]
            WB = [sb(f"WB{p}", [P, G, H], fp32, c) for p in range(2)]
            EH = [sb(f"EH{p}", [P, KB, G, P], fp32r, c) for p in range(2)]
            EL = [sb(f"EL{p}", [P, KB, G, P], fp32r, c) for p in range(2)]
            UB = [sb(f"UB{p}", [P, G, H], fp32, c) for p in range(2)]
            ZN = [sb(f"ZN{p}", [P, G, H], fp32, c) for p in range(2)]
            BI = [sb(f"BI{p}", [P, G, H], fp32, c) for p in range(2)]
            AX_ = [sb(f"AX{p}", [P, G, H], fp32, c) for p in range(2)]
            BO = [sb(f"BO{p}", [P, G, H], fp32, c) for p in range(2)]
            XO = [sb(f"XO{p}", [P, G, H], fp32, c) for p in range(2)]
            RI = [AX_[p][:, :, 0:D] for p in range(2)]
            Y2 = [sb(f"Y2_{p}", [P, G, D], fp32, c) for p in range(2)]
            YO = [BO[p][:, :, 0:D] for p in range(2)]
            en2 = [sb(f"en2_{p}", [P, G], fp32, c) for p in range(2)]
            ecl = [sb(f"ecl{p}", [P, G], fp32, c) for p in range(2)]
            ert = [sb(f"ert{p}", [P, G], fp32, c) for p in range(2)]
            eS = [sb(f"eS{p}", [P, G], fp32, c) for p in range(2)]
            eSD = [sb(f"eSD{p}", [P, G], fp32, c) for p in range(2)]
            est = [sb(f"est{p}", [P, G, 6], fp32, c) for p in range(2)]
            emv = [sb(f"emv{p}", [P, G, 2], fp32, c) for p in range(2)]
            AB = [pb(f"AB{p}", [P, G, 512], fp32, c) for p in range(2)]
            TB2 = [pb(f"TB2_{p}", [P, KB, G, P], fp32, c) for p in range(2)]
            MB2 = [pb(f"MB2_{p}", [P, G, H], fp32, c) for p in range(2)]

            seg_in = sem("seg_in", c)
            zt_in = [sem(f"zt_in{p}", c) for p in range(2)]
            idx_staged = sem("idx_staged", c)
            src_in = [sem(f"src_in{r}", c) for r in range(RING)]
            same = sem("same", c)
            goes_on = sem("goes_on", c)
            summed = sem("summed", c)
            carried = sem("carried", c)
            own_added = sem("own_added", c)
            e_transposed = sem("e_transposed", c)
            e_high = sem("e_high", c)
            e_low = sem("e_low", c)
            e_product = sem("e_product", c)
            e_early = sem("e_early", c)
            e_squared = sem("e_squared", c)
            e_varied = sem("e_varied", c)
            bias_added = sem("bias_added", c)
            e_root = sem("e_root", c)
            e_recip = sem("e_recip", c)
            e_scale = sem("e_scale", c)
            e_own = sem("e_own", c)
            ztil = sem("ztil", c)
            rk_step = sem("rk_step", c)
            rk_done = sem("rk_done", c)
            y2_done = sem("y2_done", c)
            zt_out = [sem(f"zt_out{p}", c) for p in range(2)]
            bo_out = [sem(f"bo_out{p}", c) for p in range(2)]
            xo_out = [sem(f"xo_out{p}", c) for p in range(2)]
            bi_in = [sem(f"bi_in{p}", c) for p in range(2)]
            ax_in = [sem(f"ax_in{p}", c) for p in range(2)]
            scat_idx = sem("scat_idx", c)
            scat = [sem(f"scat{p}", c) for p in range(2)]

            block = c.enter_context(nc.Block())

            LEAD, FIRST, BODY = 5, 4, (UNITS - 9) // RING * RING
            PEELED = FIRST + 2

            def positions(eng, at):
                for u in range(-LEAD, FIRST):
                    at(u, u % RING, lambda off, u=u: 0 <= u + off < UNITS)
                with eng.Fori(0, BODY // RING) as i:
                    for n in range(RING):
                        at(i * RING + (FIRST + n), (FIRST + n) % RING, lambda off: True)
                for u in range(FIRST + BODY, UNITS + 2):
                    at(u, u % RING, lambda off, u=u: 0 <= u + off < UNITS)

            def wait(eng, s_, value):
                if not isinstance(value, int) or value > 0:
                    eng.wait_ge(s_, value)

            def wait_apart(eng, s_, value):
                if not isinstance(value, int) or value > 0:
                    eng.wait_ge(s_, value)
                    eng.sem_inc(waited, 1)

            def slot_rows(t, u, first=SLOT_ROW0):
                return t[bass.ds(u * (G * P) + first, G * P), :].rearrange("(g p) f -> p g f", p=P)

            HALF = UNITS // 2
            NORM_L = [0] + F1_STEPS
            RK_L = [0, 2, 4, 6]
            BASE_IO = {0: (None, 0), 2: (0, 1), 4: (1, 0), 6: (0, 1), 8: (1, None)}

            def done_before(layers, s):
                return sum(1 for x_ in layers if x_ < s) * HALF

            BI_L, AX_L, BO_L, XO_L = [2, 4, 6, 8], [2, 4, 6, 9], [0, 2, 4, 6], [0, 4]

            @block.sync
            def _(sp):
                sp.dma_start(seg_bc[:, :], seg_dram.rearrange("(a t) p -> a (t p)", a=1).to_broadcast([P, ET * P])).then_inc(seg_in, 16)

                own = tables[0][SLOT_ROW0:SLOT_ROW0 + E_PAD, :].rearrange("(t p) f -> p t f", p=P)
                for part, (t0, t1) in enumerate(((0, PEELED * G), (PEELED * G, ET))):
                    sp.dma_start(ZT[:, t0:t1, 0:D], own[:, t0:t1]).then_inc(zt_in[part], 16)
                for s in range(STEPS):
                    for p in range(2):
                        wait(sp, bo_out[p], 16 * done_before(BO_L, s))
                        wait(sp, xo_out[p], 16 * done_before(XO_L, s))

                    def loads(u, p):
                        if s in BI_L:
                            sp.dma_start(BI[p][:, :, :], slot_rows(base_dram[BASE_IO[s][0]], u, 0)).then_inc(bi_in[p], 16)
                        if s in (2, 4, 6):
                            sp.dma_start(AX_[p][:, :, :], slot_rows(q_dram if s == 6 else xb_dram, u, 0)).then_inc(ax_in[p], 16)
                        if s == STEPS - 1:
                            sp.dma_start(RI[p], slot_rows(resid_dram, u, 0)).then_inc(ax_in[p], 16)

                    def stores(u, p):
                        q = u + s * UNITS
                        if s < STEPS - 1:
                            sp.wait_ge(ztil, q + 1)
                            sp.dma_start(slot_rows(tables[s + 1], u), ZT[:, bass.ds(u * G, G), :]).then_inc(zt_out[p], 16)
                        if s in RK_L:
                            sp.wait_ge(rk_done, u + (RK_L.index(s) * UNITS + 1))
                            sp.dma_start(slot_rows(base_dram[BASE_IO[s][1]], u, 0), BO[p][:, :, :]).then_inc(bo_out[p], 16)
                            if s in XO_L:
                                if s == 0:
                                    sp.wait_ge(bias_added, u + 1)
                                sp.dma_start(slot_rows(q_dram if s else xb_dram, u, 0), XO[p][:, :, :]).then_inc(xo_out[p], 16)
                        if s == STEPS - 1:
                            sp.wait_ge(e_early, q + 1)

                    loads(0, 0)
                    loads(1, 1)
                    with sp.Fori(0, HALF - 1) as i:
                        for p in range(2):
                            stores(i * 2 + p, p)
                            if s == 8:
                                sp.wait_ge(e_early, i * 2 + (p + s * UNITS + 1))
                            loads(i * 2 + (p + 2), p)
                    for p in range(2):
                        stores(UNITS - 2 + p, p)
                for p in range(2):
                    sp.wait_ge(zt_out[p], 16 * HALF * (STEPS - 1))

            @block.gpsimd
            def _(pool):
                pool.memset(CR[1][:, :], 0.0).then_inc(carried, 1)

                for s in range(STEPS):
                    w = D if s == 0 else H
                    for p in range(2):
                        wait(pool, zt_out[p], 16 * HALF * s)

                    def gather(u, r):
                        q = u + s * UNITS
                        if s == 0 or not isinstance(u, int) or u >= RING:
                            wait_apart(pool, summed, q * 2 - 2 * (RING - 1))
                        else:
                            wait_apart(pool, summed, s * UNITS * 2)
                        nc.gpsimd.tensor_copy(idx[r][:, :], src_row[:, bass.ds(u * G, G)]).then_inc(idx_staged, 1)
                        wait_apart(pool, idx_staged, q + 1)
                        for g in range(G):
                            pool.indirect_dma_start(out=GA[r][:, g, 0:w], out_offset=None, in_=tables[s],
                                                    in_offset=bass.IndirectOffsetOnAxis(ap=idx[r][:, g:g + 1], axis=0)
                                                    ).then_inc(src_in[r], 16)

                    def bias_sum(u, p, of):
                        wait(pool, xo_out[p], (u - p) * 8 + 16 * done_before(XO_L, s))
                        nc.gpsimd.tensor_tensor(XO[p][:, :, :], of[p][:, :, :],
                                                bf2_half[:, :, :].to_broadcast([P, G, H]), ALU.add).then_inc(bias_added, 1)

                    def scatter(u, p):
                        wait_apart(pool, scat[p], (u - p) * 16)
                        nc.gpsimd.tensor_copy(oidx[p][:, :], out_idx[:, bass.ds(u * G, G)]).then_inc(scat_idx, 1)
                        wait_apart(pool, scat_idx, u + 1)
                        wait_apart(pool, y2_done, u + 1)
                        for g in range(G):
                            pool.indirect_dma_start(out=out, out_offset=bass.IndirectOffsetOnAxis(ap=oidx[p][:, g:g + 1], axis=0),
                                                    in_=YO[p][:, g, :], in_offset=None,
                                                    bounds_check=N - 1, oob_is_err=False).then_inc(scat[p], 16)

                    def at(u, r, there):
                        p = r % 2
                        if there(5):
                            gather(u + 5, (r + 5) % RING)
                        if s == STEPS - 1 and there(-2):
                            scatter(u - 2, p)
                        if s == 0 and there(-1):
                            pool.wait_ge(e_scale, u)
                            bias_sum(u - 1, 1 - p, ZN)
                        if s == 4 and there(0):
                            pool.wait_ge(ax_in[p], (u - p) * 8 + 16 * (done_before(AX_L, s) + 1))
                            bias_sum(u, p, AX_)

                    positions(pool, at)
                for p in range(2):
                    pool.wait_ge(scat[p], 32 * HALF)

            @block.tensor
            def _(pe):
                for s in range(STEPS):
                    w = D if s == 0 else H
                    n = D if s == STEPS - 1 else H
                    hi, lo = weights[s]
                    nb = 1 if s == 0 else KB

                    def sums(u, v, g):
                        nc.tensor.matmul(AB[v % 2][:, g, 0:w], SM[v % 2][:, g, :], GA[v][:, g, 0:w], start=True, stop=False)

                    def carried_in(u, p, g):
                        pe.wait_ge(carried, (u + s * UNITS) * 2 + (g + 1))
                        nc.tensor.matmul(AB[p][:, g, 0:w], M0[p][0:1, g, :], CR[1 - g][0:1, 0:w],
                                         start=False, stop=True).then_inc(summed, 1)

                    def transposes(u, p):
                        pe.wait_ge(own_added, u + (s * UNITS + 1))
                        for g in range(G):
                            for b in range(nb):
                                mm = transpose(TB2[p][:, b, g, :], WB[p][:, g, b * P:(b + 1) * P])
                        mm.then_inc(e_transposed, 1)

                    def products(u, p, g):
                        q = u + s * UNITS
                        if g == 0:
                            pe.wait_ge(e_low, q + 1)
                            wait(pe, e_early, q - 1)
                        terms = [(a, w_, b) for b in range(nb)
                                 for a, w_ in ((EL[p], hi), (EH[p], lo), (EH[p], hi))]
                        if s == STEPS - 1:
                            mm = last_product(MB2[p][:, g, :], lambda b: EH[p][:, b, g, :], lambda b: EL[p][:, b, g, :])
                            terms = []
                        for m, (a, w_, b) in enumerate(terms):
                            mm = nc.tensor.matmul(MB2[p][:, g, 0:n], a[:, b, g, :], w_[:, b, :],
                                                  start=m == 0, stop=m == len(terms) - 1)
                        if g == G - 1:
                            mm.then_inc(e_product, 1)

                    def at(u, r, there):
                        p = r % 2
                        if there(1):
                            transposes(u + 1, 1 - p)
                        if there(0):
                            products(u, p, 0)
                        if there(3):
                            q = u + (s * UNITS + 3)
                            v = (r + 3) % RING
                            rounds = s * len(range(v, UNITS, RING))
                            pe.wait_ge(src_in[v], (u + 3 - v) * (32 // RING) + (rounds + 1) * 32)
                            pe.wait_ge(same, q + 1)
                            pe.wait_ge(goes_on, q + 1)
                            wait(pe, own_added, q - 1)
                            wait(pe, carried, q * 2 - 1)
                            sums(u + 3, v, 0)
                            carried_in(u + 3, 1 - p, 0)
                            sums(u + 3, v, 1)
                        if there(0):
                            products(u, p, 1)
                        if there(3):
                            carried_in(u + 3, 1 - p, 1)

                    positions(pe, at)

            @block.scalar
            def _(act):
                act.wait_ge(seg_in, 16)
                for s in range(STEPS):
                    w = D if s == 0 else H
                    nb = 1 if s == 0 else KB

                    def continued(u, p):
                        wait_apart(act, summed, (u + s * UNITS) * 2 - 2)
                        nc.scalar.activation(M0[p][:, :, :].rearrange("a g p -> a (g p)"),
                                             seg_bc[0:1, bass.ds(u * (G * P), G * P)],
                                             ACT.Relu, scale=-1.0, bias=1.0).then_inc(goes_on, 1)

                    def keep(u, p, g):
                        act.wait_ge(summed, (u + s * UNITS) * 2 + (g + 1))
                        nc.scalar.copy(CR[g][0:1, 0:w], AB[p][0:1, g, 0:w]).then_inc(carried, 1)

                    def scaled(u, p):
                        q = u + s * UNITS
                        if s in NORM_L:
                            wait_apart(act, e_scale, u + (NORM_L.index(s) * UNITS + 1))
                        else:
                            wait_apart(act, e_early, q + 1)
                        for g in range(G):
                            if s in F1_STEPS:
                                of, by = UB[p][:, g, :], eSD[p][:, g:g + 1]
                            else:
                                of, by = ZN[p][:, g, :], dinv[:, bass.ds(u * G + g, 1)]
                            ins = nc.scalar.activation(ZT[:, bass.ds(u * G + g, 1), :].rearrange("p a f -> p (a f)"),
                                                       of, ACT.Copy, scale=by)
                        ins.then_inc(ztil, 1)

                    def squares(u, p):
                        n = u + (NORM_L.index(s) * UNITS + 1)
                        act.wait_ge(e_early, u + (s * UNITS + 1))
                        unused = ZN if s else BI
                        for g in range(G):
                            ins = nc.scalar.activation(unused[p][:, g, :], UB[p][:, g, :], ACT.Square,
                                                       accum_out=en2[p][:, g:g + 1])
                        ins.then_inc(e_squared, 1)
                        act.wait_ge(e_squared, n)
                        nc.scalar.activation(ert[p][:, :], en2[p][:, :], ACT.Sqrt).then_inc(e_root, 1)

                    def at(u, r, there):
                        p = r % 2
                        o = 1 - p
                        if there(1):
                            act.wait_ge(e_transposed, u + (s * UNITS + 2))
                            nc.scalar.copy(EH[o][:, 0:nb], TB2[o][:, 0:nb]).then_inc(e_high, 1)
                        if there(-1) and s in NORM_L:
                            squares(u - 1, o)
                        if there(-1) and s == STEPS - 1:
                            act.wait_ge(e_varied, u)
                            nc.scalar.activation(ert[o][:, :], ecl[o][:, :], ACT.Sqrt).then_inc(e_root, 1)
                        if there(3):
                            keep(u + 3, o, 0)
                        if there(4):
                            continued(u + 4, p)
                        if there(-1) and s < STEPS - 1:
                            scaled(u - 1, o)
                        if there(3):
                            keep(u + 3, o, 1)

                    positions(act, at)

            @block.vector
            def _(dve):
                dve.wait_ge(seg_in, 16)
                for s in range(STEPS):
                    w = D if s == 0 else H
                    nb = 1 if s == 0 else KB

                    def matrices(u, p):
                        wait(dve, summed, (u + s * UNITS) * 2 - 2)
                        for g in range(G):
                            ins = nc.vector.tensor_scalar(SM[p][:, g, :], seg_bc[:, bass.ds(u * (G * P) + g * P, P)],
                                                          seg_col[:, bass.ds(u * G + g, 1)], None, ALU.is_equal)
                        ins.then_inc(same, 1)

                    def add_own(u, p):
                        q = u + s * UNITS
                        dve.wait_ge(carried, q * 2 + 3)
                        wait(dve, e_transposed, q - 1)
                        if s == 0:
                            dve.wait_ge(zt_in[int(not isinstance(u, int) or u >= PEELED)], 16)
                        else:
                            dve.wait_ge(ztil, q + (1 - UNITS))
                        nc.vector.tensor_tensor(WB[p][:, :, 0:w], AB[p][:, :, 0:w], ZT[:, bass.ds(u * G, G), 0:w],
                                                ALU.add).then_inc(own_added, 1)

                    def early(u, p):
                        q = u + s * UNITS
                        dve.wait_ge(e_product, q + 1)
                        if s < STEPS - 1:
                            wait(dve, ztil, q - 1)
                        for g in range(G):
                            col = bass.ds(u * G + g, 1)
                            if s in NORM_L:
                                ins = nc.vector.scalar_tensor_tensor(
                                    out=UB[p][:, g, :], in0=MB2[p][:, g, :], scalar=dinv[:, col],
                                    in1=(bf1_bc if s else b1_bc)[:, :], op0=ALU.mult, op1=ALU.add)
                            elif s < STEPS - 1:
                                if g == 0:
                                    dve.wait_ge(bi_in[p], (u - p) * 8 + 16 * (done_before(BI_L, s) + 1))
                                ins = nc.vector.scalar_tensor_tensor(
                                    out=ZN[p][:, g, :], in0=MB2[p][:, g, :], scalar=dinv[:, col],
                                    in1=BI[p][:, g, :], op0=ALU.mult, op1=ALU.add)
                            else:
                                if g == 0:
                                    dve.wait_ge(ax_in[p], (u - p) * 8 + 16 * (done_before(AX_L, s) + 1))
                                ins = nc.vector.scalar_tensor_tensor(
                                    out=Y2[p][:, g, :], in0=MB2[p][:, g, 0:D], scalar=dinv_half[:, col],
                                    in1=RI[p][:, g, :], op0=ALU.mult, op1=ALU.add)
                        if s == STEPS - 1:
                            ins.then_inc(e_own, 1)
                            dve.wait_ge(e_own, u * 4 + 1)
                            for g in range(G):
                                ins = nc.vector.scalar_tensor_tensor(
                                    out=Y2[p][:, g, :], in0=MB2[p][:, g, D:2 * D], scalar=dinv_half[:, bass.ds(u * G + g, 1)],
                                    in1=Y2[p][:, g, :], op0=ALU.mult, op1=ALU.add)
                        ins.then_inc(e_early, 1)

                    def variance(u, p):
                        dve.wait_ge(e_early, u + (s * UNITS + 1))
                        for g in range(G):
                            ins = nc.vector.bn_stats(est[p][:, g, :], Y2[p][:, g, :])
                        ins.then_inc(e_own, 1)
                        wait_apart(dve, e_own, u * 4 + 2)
                        for g in range(G):
                            ins = nc.vector.bn_aggr(emv[p][:, g, :], est[p][:, g, :])
                        ins.then_inc(e_own, 1)
                        dve.wait_ge(e_own, u * 4 + 3)
                        nc.vector.tensor_scalar_add(ecl[p][:, :], emv[p][:, :, 1], EPS_LN).then_inc(e_varied, 1)

                    def scale(u, p):
                        n = u + (NORM_L.index(s) * UNITS + 1)
                        dve.wait_ge(e_root, n)
                        nc.vector.tensor_scalar(ecl[p][:, :], ert[p][:, :], EPS_NORM, 1.0 / COEF.get(s, 1.0),
                                                ALU.max, ALU.mult).then_inc(e_recip, 1)
                        dve.wait_ge(e_recip, n * 2 - 1)
                        nc.vector.reciprocal(eS[p][:, :], ecl[p][:, :]).then_inc(e_recip, 1)
                        dve.wait_ge(e_recip, n * 2)
                        if s:
                            nc.vector.tensor_tensor(eSD[p][:, :], eS[p][:, :], dinv[:, bass.ds(u * G, G)],
                                                    ALU.mult).then_inc(e_scale, 1)
                        else:
                            wait(dve, bias_added, u - 1)
                            for g in range(G):
                                ins = nc.vector.tensor_scalar(ZN[p][:, g, :], UB[p][:, g, :], eS[p][:, g:g + 1],
                                                              None, ALU.mult)
                            ins.then_inc(e_scale, 1)

                    def late(u, p):
                        if s in RK_L:
                            n = RK_L.index(s) * UNITS
                            wait(dve, bo_out[p], (u - p) * 8 + 16 * done_before(BO_L, s))
                            if s in (2, 4, 6):
                                dve.wait_ge(e_early, u + (s * UNITS + 1))
                                dve.wait_ge(ax_in[p], (u - p) * 8 + 16 * (done_before(AX_L, s) + 1))
                            if s == 0:
                                dve.wait_ge(e_scale, u + 1)
                                nc.vector.scalar_tensor_tensor(out=BO[p][:, :, :], in0=ZN[p][:, :, :], scalar=1.5,
                                                               in1=bf2_half[:, :, :].to_broadcast([P, G, H]),
                                                               op0=ALU.mult, op1=ALU.add).then_inc(rk_done, 1)
                            elif s == 2:
                                nc.vector.scalar_tensor_tensor(out=BO[p][:, :, :], in0=ZN[p][:, :, :], scalar=0.5,
                                                               in1=AX_[p][:, :, :], op0=ALU.mult, op1=ALU.add).then_inc(rk_done, 1)
                            elif s == 4:
                                dve.wait_ge(bias_added, u + (UNITS + 1))
                                nc.vector.tensor_tensor(BO[p][:, :, :], ZN[p][:, :, :], XO[p][:, :, :], ALU.add).then_inc(rk_step, 1)
                                dve.wait_ge(rk_step, u * 2 + 1)
                                nc.vector.tensor_tensor(XO[p][:, :, :], BI[p][:, :, :], BO[p][:, :, :], ALU.add).then_inc(rk_step, 1)
                                dve.wait_ge(rk_step, u * 2 + 2)
                                nc.vector.scalar_tensor_tensor(out=XO[p][:, :, :], in0=AX_[p][:, :, :], scalar=-2.5,
                                                               in1=XO[p][:, :, :], op0=ALU.mult, op1=ALU.add).then_inc(rk_done, 1)
                            elif s == 6:
                                nc.vector.scalar_tensor_tensor(out=BO[p][:, :, :], in0=AX_[p][:, :, :], scalar=4.0 / 3.0,
                                                               in1=ZN[p][:, :, :], op0=ALU.mult, op1=ALU.add).then_inc(rk_done, 1)
                        if s == STEPS - 1:
                            dve.wait_ge(e_root, u + (len(NORM_L) * UNITS + 1))
                            nc.vector.reciprocal(eS[p][:, :], ert[p][:, :]).then_inc(e_own, 1)
                            dve.wait_ge(e_own, u * 4 + 4)
                            wait(dve, scat[p], (u - p) * 16)
                            for g in range(G):
                                ins = nc.vector.tensor_scalar(YO[p][:, g, :], Y2[p][:, g, :], emv[p][:, g, 0:1],
                                                              eS[p][:, g:g + 1], ALU.subtract, ALU.mult)
                            ins.then_inc(y2_done, 1)

                    def at(u, r, there):
                        p = r % 2
                        o = 1 - p
                        if there(2):
                            add_own(u + 2, p)
                        if there(-1) and s == STEPS - 1:
                            variance(u - 1, o)
                        if there(1):
                            dve.wait_ge(e_high, u + (s * UNITS + 2))
                            nc.vector.tensor_tensor(EL[o][:, 0:nb], TB2[o][:, 0:nb], EH[o][:, 0:nb].bitcast(fp32),
                                                    ALU.subtract).then_inc(e_low, 1)
                        if there(-1) and s in NORM_L:
                            scale(u - 1, o)
                        if there(4):
                            matrices(u + 4, p)
                        if there(-1):
                            late(u - 1, o)
                        if there(0):
                            early(u, p)

                    positions(dve, at)


_INS = ['x', 'src_pad', 'dst_pad', 'W1', 'b1', 'Wf1', 'bf1', 'Wf2', 'bf2', 'W2', 'b2']
_OUTS = [((50000, 128), 'float32')]


def laid_out(inputs):
    import numpy as _np

    named = {n.removeprefix('L0_gnn_'): _np.asarray(a) for n, a in inputs.items()}
    edges, nodes = named['src'].shape[0], named['x'].shape[0]
    padded = -(-edges // 512) * 512
    named['src_pad'] = _np.concatenate([named.pop('src'), _np.zeros(padded - edges, _np.int32)])
    named['dst_pad'] = _np.concatenate([_np.full(1, -1, _np.int32), named.pop('dst'),
                                        _np.full(padded - edges, nodes, _np.int32), _np.full(1, -1, _np.int32)])
    return named


def kernel(**inputs):
    import numpy as _np
    import concourse.bacc as _bacc
    from concourse import mybir as _mybir
    from concourse.bass_utils import run_bass_kernel_spmd as _run

    named = laid_out(inputs)
    nc = _bacc.Bacc("TRN2", target_bir_lowering=False, num_devices=1)
    arrays, args = {}, []
    for name in _INS:
        a = _np.ascontiguousarray(named[name])
        arrays[f"in_{name}_dram"] = a
        args.append(nc.dram_tensor(f"in_{name}_dram", a.shape, _mybir.dt.from_np(a.dtype), kind="ExternalInput").ap())
    for i, (shape, dtype) in enumerate(_OUTS):
        dt = _mybir.dt.from_np(_np.dtype(dtype))
        args.append(nc.dram_tensor(f"out_{i}_dram", shape, dt, kind="ExternalOutput").ap())
    bass_gnn_rk4_resnorm(nc, *args)
    r = _run(nc, [arrays], core_ids=[0])
    return r.results[0]["out_0_dram"]
```
